# Optimizing a Trainium2 kernel written in Bass

```python
import numpy as np
import jax
import jax.numpy as jnp

def _softmax(x, axis=-1):
    return jax.nn.softmax(x, axis=axis)

def _gelu(x):
    return jax.nn.gelu(x, approximate=True)

def _silu(x):
    return jax.nn.silu(x)

def _sigmoid(x):
    return jax.nn.sigmoid(x)

def _layernorm(x, axis=-1, eps=1e-05):
    m = jnp.mean(x, axis=axis, keepdims=True)
    v = jnp.var(x, axis=axis, keepdims=True)
    return (x - m) / jnp.sqrt(v + eps)

def _scatter_add(tgt, idx, src, axis=0):
    return tgt.at[idx].add(src)

def _segment_sum(src, seg, n):
    return jax.ops.segment_sum(src, seg, n)
kernel_name = 'mk_gnn_ffn_d1_gnn_r8_190ec1'

def setup_inputs(seed: int=0):
    np.random.seed(seed)
    _w = jnp.asarray

    def _rec_inputs():
        import jax
        import jax.numpy as jnp
        _gk = jax.random.key(seed)
        x = -0.0002117 + 1 * jax.random.normal(jax.random.fold_in(_gk, 1), (12500, 256), jnp.float32)
        _s = jax.random.randint(jax.random.fold_in(_gk, 2), (100000,), 0, 12500, jnp.int32)
        _d = jax.random.randint(jax.random.fold_in(_gk, 3), (100000,), 0, 12500, jnp.int32)
        _loop = jnp.arange(12500, dtype=jnp.int32)
        src = jnp.concatenate([_s, _d, _loop])
        dst = jnp.concatenate([_d, _s, _loop])
        _o = jnp.argsort(dst, stable=True)
        src = src[_o]
        dst = dst[_o]
        edge_weight = jax.random.uniform(jax.random.fold_in(_gk, 12), (212500,), jnp.float32, 0.0, 1)
        return (x, src, dst, edge_weight)
    x, src, dst, edge_weight = _rec_inputs()

    def _L0_gnn_setup():
        import jax, jax.numpy as jnp
        import numpy as np
        N = 12500
        E = 400000
        F = 256
        EPS = 1e-05

        def _spmm_plus_eye(rows, cols, vals, X):
            msgs = vals[:, None] * X[cols]
            agg = jax.ops.segment_sum(msgs, rows, num_segments=N)
            return agg + X

        def _batchnorm_relu(x, gamma, beta):
            mean = jnp.mean(x, axis=0)
            var = jnp.mean(jnp.square(x - mean), axis=0)
            xn = (x - mean) * jax.lax.rsqrt(var + EPS)
            return jax.nn.relu(xn * gamma + beta)
        key = jax.random.key(seed)
        k1, k2, k3, k4, k5, k6 = jax.random.split(key, 6)
        stdv = 1.0 / np.sqrt(F)
        return {'feature': jax.random.normal(k1, (N, F), dtype=jnp.float32), 'rows': jax.random.randint(k2, (E,), 0, N, dtype=jnp.int32), 'cols': jax.random.randint(k3, (E,), 0, N, dtype=jnp.int32), 'vals': jax.random.uniform(k4, (E,), dtype=jnp.float32), 'W1': jax.random.uniform(k5, (F, F), jnp.float32, -stdv, stdv), 'W2': jax.random.uniform(k6, (F, F), jnp.float32, -stdv, stdv), 'gamma': jnp.ones((F,), jnp.float32), 'beta': jnp.zeros((F,), jnp.float32)}
    _L0_gnn_all = _L0_gnn_setup()
    _L0_gnn_in = {k: v for k, v in _L0_gnn_all.items() if k in ('W1', 'W2', 'gamma', 'beta')}
    del _L0_gnn_all

    def _L0_ffn_setup():
        import jax, jax.numpy as jnp
        import numpy as np
        NUM_EXPERTS = 8
        TOP_K = 2
        B, S, D = (8, 1024, 256)

        def _moe(tokens, router_w, w1, b1, w2, b2):
            N = tokens.shape[0]
            E = router_w.shape[0]
            logits = tokens.astype(jnp.float32) @ router_w.astype(jnp.float32).T
            probs = jax.nn.softmax(logits, axis=-1)
            rw, re = jax.lax.top_k(probs, TOP_K)
            if TOP_K > 1:
                rw = rw / jnp.maximum(rw.sum(-1, keepdims=True), 1e-12)
            rw = rw.astype(tokens.dtype)
            combine = jnp.zeros((N, E), tokens.dtype).at[jnp.arange(N)[:, None], re].set(rw)
            out = tokens
            for e in range(E):
                h = jax.nn.gelu(tokens @ w1[e] + b1[e], approximate=False)
                y = h @ w2[e] + b2[e]
                out = out + combine[:, e:e + 1] * y
            return out
        key = jax.random.key(seed)
        ks = jax.random.split(key, 4)
        scale = 1.0 / np.sqrt(D).astype(np.float32)
        return {'input_embeddings': jax.random.normal(ks[0], (B, S, D), jnp.float32), 'router_w': jax.random.normal(ks[1], (NUM_EXPERTS, D), jnp.float32) * scale, 'w1': jax.random.normal(ks[2], (NUM_EXPERTS, D, D), jnp.float32) * scale, 'b1': jnp.zeros((NUM_EXPERTS, D), jnp.float32), 'w2': jax.random.normal(ks[3], (NUM_EXPERTS, D, D), jnp.float32) * scale, 'b2': jnp.zeros((NUM_EXPERTS, D), jnp.float32)}
    _L0_ffn_all = _L0_ffn_setup()
    _L0_ffn_in = {k: v for k, v in _L0_ffn_all.items() if k in ('router_w', 'w1', 'b1', 'w2', 'b2')}
    del _L0_ffn_all
    return {'x': x, 'src': src, 'dst': dst, 'edge_weight': edge_weight, 'L0_gnn_W1': _L0_gnn_in['W1'], 'L0_gnn_W2': _L0_gnn_in['W2'], 'L0_gnn_gamma': _L0_gnn_in['gamma'], 'L0_gnn_beta': _L0_gnn_in['beta'], 'L0_ffn_router_w': _L0_ffn_in['router_w'], 'L0_ffn_w1': _L0_ffn_in['w1'], 'L0_ffn_b1': _L0_ffn_in['b1'], 'L0_ffn_w2': _L0_ffn_in['w2'], 'L0_ffn_b2': _L0_ffn_in['b2']}

def reference(x, src, dst, edge_weight, L0_gnn_W1, L0_gnn_W2, L0_gnn_gamma, L0_gnn_beta, L0_ffn_router_w, L0_ffn_w1, L0_ffn_b1, L0_ffn_w2, L0_ffn_b2):
    import jax
    import jax.numpy as jnp

    def _L0_gnn_ref(feature, rows, cols, vals, W1, W2, gamma, beta):
        import jax, jax.numpy as jnp
        import numpy as np
        N = 12500
        E = 400000
        F = 256
        EPS = 1e-05

        def _spmm_plus_eye(rows, cols, vals, X):
            msgs = vals[:, None] * X[cols]
            agg = jax.ops.segment_sum(msgs, rows, num_segments=N)
            return agg + X

        def _batchnorm_relu(x, gamma, beta):
            mean = jnp.mean(x, axis=0)
            var = jnp.mean(jnp.square(x - mean), axis=0)
            xn = (x - mean) * jax.lax.rsqrt(var + EPS)
            return jax.nn.relu(xn * gamma + beta)
        support = feature @ W1
        out = _spmm_plus_eye(rows, cols, vals, support)
        out = _batchnorm_relu(out, gamma, beta)
        out = _spmm_plus_eye(rows, cols, vals, out @ W2)
        return out

    def _L0_ffn_ref(input_embeddings, router_w, w1, b1, w2, b2):
        import jax, jax.numpy as jnp
        import numpy as np
        NUM_EXPERTS = 8
        TOP_K = 2
        B, S, D = (8, 1024, 256)

        def _moe(tokens, router_w, w1, b1, w2, b2):
            N = tokens.shape[0]
            E = router_w.shape[0]
            logits = tokens.astype(jnp.float32) @ router_w.astype(jnp.float32).T
            probs = jax.nn.softmax(logits, axis=-1)
            rw, re = jax.lax.top_k(probs, TOP_K)
            if TOP_K > 1:
                rw = rw / jnp.maximum(rw.sum(-1, keepdims=True), 1e-12)
            rw = rw.astype(tokens.dtype)
            combine = jnp.zeros((N, E), tokens.dtype).at[jnp.arange(N)[:, None], re].set(rw)
            out = tokens
            for e in range(E):
                h = jax.nn.gelu(tokens @ w1[e] + b1[e], approximate=False)
                y = h @ w2[e] + b2[e]
                out = out + combine[:, e:e + 1] * y
            return out
        b, s, d = input_embeddings.shape
        tokens = input_embeddings.reshape(b * s, d)
        return _moe(tokens, router_w, w1, b1, w2, b2).reshape(b, s, d)
    x = x + _L0_gnn_ref(_layernorm(x, axis=-1), src, dst, edge_weight, L0_gnn_W1, L0_gnn_W2, L0_gnn_gamma, L0_gnn_beta)
    x = x + _L0_ffn_ref(_layernorm(x, axis=-1)[None], L0_ffn_router_w, L0_ffn_w1, L0_ffn_b1, L0_ffn_w2, L0_ffn_b2)[0]
    return x

_drawn_inputs = setup_inputs


def setup_inputs(seed=0):
    import zlib

    import numpy as np

    out = dict(_drawn_inputs(seed))
    spreads = {'L0_gnn_gamma': (1.0, 0.2),
     'L0_gnn_beta': (0.0, 0.1),
     'L0_ffn_b1': (0.0, 0.675),
     'L0_ffn_b2': (0.0, 0.457)}
    factors = {}
    for name, (base, spread) in spreads.items():
        noise = np.random.default_rng([zlib.crc32(name.encode()), seed]).standard_normal(out[name].shape)
        drawn = base * np.exp(spread * noise) if base else spread * noise
        out[name] = jnp.asarray(drawn.astype(out[name].dtype))
    for name, factor in factors.items():
        out[name] = (out[name] * factor).astype(out[name].dtype)
    return out
```

```python
import concourse.bass as bass
from concourse import mybir
from contextlib import ExitStack

F32 = mybir.dt.float32
BF16 = mybir.dt.bfloat16
I32 = mybir.dt.int32
U32 = mybir.dt.uint32
ALU = mybir.AluOpType
ACT = mybir.ActivationFunctionType
AX = mybir.AxisListType

N = 12500
F = 256
E = 212500
P = 128
NB = 98
LAST = N - (NB - 1) * P
PE_P = 125
EC = 1700
GC = 5
NG = EC // GC
SG = 20
NSG = EC // SG
CH = (E + NB * 127) // 128
NCOL = 1760
XB = 14
NX = 7
SB = 4
SBS = [(b, min(SB, NB - b)) for b in range(0, NB, SB)]
NEXP = 8
EPS = 1e-05
GR = 12
SR = 6
PR = 8
RL = 8


class Queues:

    def __init__(self, nc, ctx):
        self.nc, self.ctx = nc, ctx
        self.q = {"sync": [], "scalar": [], "vector": [], "tensor": [], "gpsimd": []}
        self.sems, self.count, self.passed = {}, {}, {}

    def sem(self, name):
        if name not in self.sems:
            self.sems[name] = self.ctx.enter_context(self.nc.semaphore(name))
            self.count[name] = 0
        return self.sems[name]

    def wait(self, eng, *marks):
        for name, value in marks:
            if self.passed.get((eng, name), 0) < value:
                self.passed[(eng, name)] = value
                s = self.sem(name)
                self.q[eng].append(lambda e, s=s, value=value: e.wait_ge(s, value))

    def do(self, eng, fn, *marks, inc=None, by=1):
        self.wait(eng, *marks)
        if inc is None:
            self.q[eng].append(fn)
            return None
        s = self.sem(inc)
        self.count[inc] += by
        self.q[eng].append(lambda e, s=s: fn(e).then_inc(s, by))
        return inc, self.count[inc]

    def dma(self, eng, out, in_, *marks, inc):
        return self.do(eng, lambda e: e.dma_start(out, in_), *marks, inc=inc, by=16)

    def run(self, block):
        for name in self.q:
            def body(eng, name=name):
                for fn in self.q[name]:
                    fn(eng)
            {"sync": block.sync, "scalar": block.scalar, "vector": block.vector,
             "tensor": block.tensor, "gpsimd": block.gpsimd}[name](body)


def build(nc, x, src, dst, ew, W1, W2, gamma, beta, rw, w1, b1, w2, b2, out):
    h1 = nc.dram_tensor("h1", (N, F), F32, kind="Internal").ap()
    h2 = nc.dram_tensor("h2", (N, F), F32, kind="Internal").ap()
    tabd = nc.dram_tensor("tabd", (P * NCOL, 4), F32, kind="Internal").ap()
    tab_rows = tabd.rearrange("(p c) k -> p (c k)", p=P)

    with ExitStack() as ctx:
        Q = Queues(nc, ctx)
        do, dma, wait = Q.do, Q.dma, Q.wait

        def sb(name, shape, dt=F32):
            return ctx.enter_context(nc.sbuf_tensor(name, shape, dt))

        acc = sb("acc", [P, NB * F])
        R = sb("R", [P, 20480])
        ident = sb("ident", [P, P])
        iota_f = sb("iota_f", [P, P])
        W1s = sb("W1s", [P, 2, F])
        W2s = sb("W2s", [P, 2, F])
        gbT = sb("gbT", [P, 4])
        rwT = sb("rwT", [P, 2, NEXP])
        b1T = sb("b1T", [P, NEXP, 2])
        b2s = sb("b2s", [NEXP, F])
        pre = sb("pre", [36, P])
        bkI = sb("bkI", [1, NCOL], I32)
        small = sb("small", [P, 640])
        psum = [ctx.enter_context(nc.psum_tensor(f"ps{i}", [P, 512], F32)) for i in range(8)]

        def Rv(at, n, p=P):
            return R[0:p, at:at + n]

        o = 0
        srcI = Rv(o, EC, PE_P).bitcast(I32); o += EC
        bkf = Rv(o, EC, PE_P); o += EC
        rec = Rv(o, EC * 4, PE_P); o += EC * 4
        posf = Rv(o, EC, PE_P); o += EC
        posI = Rv(o, EC, PE_P).bitcast(I32); o += EC
        NBB = 3
        Bo = o
        Bt = [Rv(o + i * SG * NB // 2, SG * NB // 2, PE_P).bitcast(BF16) for i in range(NBB)]
        o += NBB * SG * NB // 2
        NDG = 4
        dg = [Rv(o + i * NB, NB, NB) for i in range(NDG)]; o += NDG * NB
        junk = [Rv(o + i * NB, NB, PE_P) for i in range(2 * GC)]; o += 2 * GC * NB
        ones = Rv(o, P, P); o += P
        lowT = Rv(o, P, P); o += P
        onesb = Rv(o, P // 2, P).bitcast(BF16); o += P // 2
        lowb = Rv(o, P // 2, P).bitcast(BF16); o += P // 2
        cum = Rv(o, NG, NB); o += NG
        gb = Rv(o, NG, NB); o += NG
        zrow = Rv(o, 704); o += 704
        assert o <= 20480, o
        s_tot = small[0:NB, 0:1]
        s_nI = small[0:NB, 1:2].bitcast(I32)
        s_n = small[0:NB, 2:3]
        s_sc = small[0:NB, 3:4]
        s_sc128 = small[0:NB, 4:5]
        posS = small[0:PE_P, 8:8 + 3 * SG].bitcast(I32)
        stats = small[:, 80:80 + XB * 6]
        mv = small[:, 168:168 + XB * 2]
        nrm = small[:, 200:200 + XB * 2]
        o = 0
        tab = Rv(o, NCOL * 4); o += NCOL * 4
        tab3 = tab.rearrange("p (c k) -> p c k", k=4)
        G = [Rv(o + i * F, F) for i in range(GR)]; o += GR * F
        S = [Rv(o + i * P, P) for i in range(SR)]; o += SR * P
        aT = [Rv(o + i * 1024, 1024) for i in range(2)]; o += 2048
        sq = [Rv(o + i * 512, 512) for i in range(2)]; o += 1024
        assert o <= 20480, o
        o = 0
        w1s = Rv(o, 4096).rearrange("p (e k f) -> p e k f", e=NEXP, k=2); o += 4096
        w2s = Rv(o, 4096).rearrange("p (e k f) -> p e k f", e=NEXP, k=2); o += 4096
        zT = [Rv(o + i * 1024, 1024) for i in range(1)]; o += 1024
        xt = [Rv(o + i * 1024, 1024) for i in range(2)]; o += 2048
        tt = [Rv(o + i * 1024, 1024) for i in range(1)]; o += 1024
        tT = [Rv(o + i * 1024, 1024) for i in range(2)]; o += 2048
        hT = [Rv(o + i * 1024, 1024) for i in range(2)]; o += 2048
        comb = [Rv(o + i * 32, 32) for i in range(2)]; o += 64
        cT = [Rv(o + i * 512, 512, NEXP) for i in range(1)]; o += 512
        rt = Rv(o, 512); o += 512
        assert o <= 20480, o

        def acc_b(b, n=1):
            return acc[:, b * F:(b + n) * F]

        m = do("gpsimd", lambda e: e.iota(iota_f[:, :].bitcast(I32), pattern=[[1, P]], base=0, channel_multiplier=0), inc="iota")
        m_iota = do("vector", lambda e: e.tensor_copy(iota_f[:, :], iota_f[:, :].bitcast(I32)), m, inc="iotaf")
        m1 = do("gpsimd", lambda e: e.memset(ident[:, :], 0.0), inc="cst")
        m2 = do("gpsimd", lambda e: e.memset(ones, 1.0), inc="cst")
        m_ident = do("gpsimd", lambda e: e.affine_select(out=ident[:, :], in_=ident[:, :], compare_op=ALU.not_equal, fill=1.0,
                     base=0, pattern=[[-1, P]], channel_multiplier=1), m2, inc="cst")
        m_low = do("gpsimd", lambda e: e.affine_select(out=lowT, in_=ones, compare_op=ALU.is_gt, fill=0.0,
                   base=0, pattern=[[1, P]], channel_multiplier=-1), m_ident, inc="cst")
        m_zrow = do("gpsimd", lambda e: e.memset(zrow, 0.0), inc="cst")
        do("vector", lambda e: e.tensor_copy(onesb, ones), m_low, inc="cstb")
        m_cstb = do("vector", lambda e: e.tensor_copy(lowb, lowT), inc="cstb")

        ld = rec
        e_src = src.rearrange("(p c) -> p c", p=PE_P)
        e_dst = dst.rearrange("(p c) -> p c", p=PE_P)
        e_w = ew.rearrange("(p c) -> p c", p=PE_P)
        rec3 = rec.rearrange("p (c k) -> p c k", k=4)
        rec3i = rec.bitcast(I32).rearrange("p (c k) -> p c k", k=4)
        m_src = dma("sync", srcI, e_src, inc="ld_src")
        m_dst = dma("sync", posI, e_dst, inc="ld_dst")
        m_ew = dma("sync", posf, e_w, inc="ld_w")
        for k in range(10):
            n0, n1 = k * 704, min((k + 1) * 704, NCOL * 4)
            m_fill = dma("sync", tab_rows[:, n0:n1], zrow[:, 0:n1 - n0], m_zrow, inc="fill")
        m = do("vector", lambda e: e.tensor_single_scalar(bkf.bitcast(I32), srcI, 7, op=ALU.logical_shift_right), m_src, inc="edg")
        m = do("vector", lambda e: e.tensor_single_scalar(srcI, srcI, 127, op=ALU.bitwise_and), m, inc="edg")
        m_bkf = do("vector", lambda e: e.tensor_copy(bkf, bkf.bitcast(I32)), m, inc="edg")
        m_r0 = do("vector", lambda e: e.tensor_copy(rec3i[:, :, 0], posI), m_dst, inc="edg")
        m_r1 = do("vector", lambda e: e.tensor_copy(rec3[:, :, 1], srcI), inc="edg")
        m_r2 = do("vector", lambda e: e.tensor_copy(rec3[:, :, 2], posf), m_ew, inc="edg")
        m_rec = do("vector", lambda e: e.memset(rec3[:, :, 3], 0.0), inc="edg")

        m_accz = do("gpsimd", lambda e: e.memset(acc_b(NB - 1), 0.0), inc="accz")
        m_x = []
        for i in range(NX):
            b0 = i * XB
            n = XB if i < NX - 1 else XB - 1
            m = dma("scalar", acc_b(b0, n).rearrange("p (b f) -> p b f", f=F),
                    x[b0 * P:(b0 + n) * P, :].rearrange("(b p) f -> p b f", p=P), inc=f"ld_x{i}")
            if i == NX - 1:
                m = dma("scalar", acc[0:LAST, (NB - 1) * F:NB * F], x[(NB - 1) * P:N, :], m_accz, inc=f"ld_x{i}")
            m_x.append(m)

        def norm_group(i):
            b0 = i * XB
            for j in range(XB):
                m = do("vector", lambda e, j=j: e.bn_stats(stats[:, 6 * j:6 * j + 6], acc_b(b0 + j)),
                       m_x[i], *([("ln_ab", i)] if i else []), inc="ln_st")
            for j in range(XB):
                m2 = do("vector", lambda e, j=j: e.bn_aggr(mv[:, 2 * j:2 * j + 2], stats[:, 6 * j:6 * j + 6]), m, inc="ln_ag")
            mv3 = mv.rearrange("p (b k) -> p b k", k=2)
            m = do("vector", lambda e: e.tensor_scalar(nrm[:, 0:XB], mv3[:, :, 1], EPS, None, ALU.add),
                   m2, *([("ln_h", XB * i)] if i else []), inc="ln_ve")
            m = do("scalar", lambda e: e.activation(nrm[:, 0:XB], nrm[:, 0:XB], ACT.Sqrt), m, inc="ln_sq")
            m = do("vector", lambda e: e.reciprocal(nrm[:, 0:XB], nrm[:, 0:XB]), m, inc="ln_rs")
            m = do("vector", lambda e: e.scalar_tensor_tensor(nrm[:, XB:2 * XB], mv3[:, :, 0], -1.0, nrm[:, 0:XB], ALU.mult, ALU.mult),
                   m, inc="ln_ab")
            for j in range(XB):
                mh = do("scalar", lambda e, j=j: e.activation(acc_b(b0 + j), acc_b(b0 + j), ACT.Identity,
                        bias=nrm[:, XB + j:XB + j + 1], scale=nrm[:, j:j + 1]), m, inc="ln_h")
            n = XB if i < NX - 1 else XB - 1
            dma("sync", h1[b0 * P:(b0 + n) * P, :].rearrange("(b p) f -> p b f", p=P),
                acc_b(b0, n).rearrange("p (b f) -> p b f", f=F), mh, inc="st_h1")
            if i == NX - 1:
                dma("sync", h1[(NB - 1) * P:N, :], acc[0:LAST, (NB - 1) * F:NB * F], mh, inc="st_h1")

        def onehot(i, name, *marks):
            c0 = (i % NSG) * SG
            Bv = Bt[i % NBB].rearrange("p (c b) -> p c b", b=NB)
            return do("vector", lambda e: e.tensor_tensor(
                Bv, bkf[:, c0:c0 + SG].rearrange("p (c o) -> p c o", o=1).broadcast_to([PE_P, SG, NB]),
                iota_f[0:PE_P, 0:NB].rearrange("p (o b) -> p o b", o=1).broadcast_to([PE_P, SG, NB]), ALU.is_equal),
                *marks, inc=name)

        cnt = psum[0][0:NB, 0:NG]
        m_cnt = {}
        for i in range(NSG):
            mb = onehot(i, "oneh", m_bkf, m_iota, *([m_cnt[i - NBB]] if i >= NBB else []))
            if i % 12 == 5 and i // 12 < NX:
                norm_group(i // 12)
            for c in range(SG):
                g, j = i * (SG // GC) + c // GC, c % GC
                fn = lambda e, i=i, c=c, g=g, j=j: e.matmul(
                    cnt[:, g:g + 1], Bt[i % NBB][:, c * NB:(c + 1) * NB], onesb[0:PE_P, 0:1], start=j == 0, stop=j == GC - 1)
                m = do("tensor", fn, mb, m_cstb, inc="cnt" if c == SG - 1 else None)
            m_cnt[i] = m
        m = do("vector", lambda e: e.tensor_tensor_scan(cum, ones[0:NB, 0:1].broadcast_to([NB, NG]), cnt, 0.0, ALU.mult, ALU.add), m, inc="base")
        m = do("vector", lambda e: e.tensor_scalar(s_tot, cum[:, NG - 1:NG], 127.0, None, ALU.add), m, inc="base")
        m = do("vector", lambda e: e.tensor_copy(s_nI, s_tot), m, inc="base")
        m = do("vector", lambda e: e.tensor_single_scalar(s_nI, s_nI, 7, op=ALU.logical_shift_right), m, inc="base")
        m = do("vector", lambda e: e.tensor_copy(s_n, s_nI), m, inc="base")
        m = do("tensor", lambda e: e.matmul(psum[1][0:NB, 0:1], lowT[0:NB, 0:NB], s_n, start=True, stop=True), m, inc="scp")
        m = do("vector", lambda e: e.tensor_copy(s_sc, psum[1][0:NB, 0:1]), m, inc="base")
        m = do("vector", lambda e: e.tensor_scalar(s_sc128, s_sc, 128.0, None, ALU.mult), m, inc="base")
        m = do("vector", lambda e: e.tensor_tensor(gb, cum, cnt, ALU.subtract), m, inc="base")
        m_gb = do("vector", lambda e: e.tensor_scalar(gb, gb, s_sc128, None, ALU.add), m, inc="base")

        m_pos, m_dg, m_rk = {}, {}, {}
        m_sel = {}
        for i in range(NSG):
            k = NSG + i
            ob = [m_cnt[k - NBB]] if k - NBB < NSG else [m_rk[(k - NBB - NSG + 1) * (SG // GC) - 1]]
            mb = onehot(k, "oneh", m_gb, *ob)
            for g in range(i * SG // GC, (i + 1) * SG // GC):
                c0 = (g * GC) % SG
                md = do("vector", lambda e, g=g: e.tensor_scalar(dg[g % NDG], ident[0:NB, 0:NB], gb[:, g:g + 1], None, ALU.mult),
                        m_gb, m_ident, *([m_rk[g - NDG]] if g >= NDG else []), inc="diag")
                bank = psum[2 + g % 6][0:PE_P, 0:GC * NB].rearrange("p (c b) -> p c b", b=NB)
                Bv = Bt[k % NBB].rearrange("p (c b) -> p c b", b=NB)
                do("tensor", lambda e, g=g, bank=bank: e.matmul(
                    bank, ones[0:NB, 0:PE_P], dg[g % NDG].rearrange("p (o b) -> p o b", o=1).broadcast_to([NB, GC, NB]),
                    start=True, stop=False), md, mb, *([m_sel[g - 6]] if g >= 6 else []))
                for j in range(GC - 1):
                    do("tensor", lambda e, j=j, bank=bank, Bv=Bv, c0=c0: e.matmul(
                        bank[:, j + 1:GC, :], onesb[0:PE_P, 0:PE_P],
                        Bv[:, c0 + j:c0 + j + 1, :].broadcast_to([PE_P, GC - 1 - j, NB]), start=False, stop=False))
                m_rk[g] = do("tensor", lambda e, bank=bank, Bv=Bv, c0=c0: e.matmul(
                    bank, lowb[0:PE_P, 0:PE_P], Bv[:, c0:c0 + GC, :], start=False, stop=True), inc="rank")

            def select(g):
                bank = psum[2 + g % 6]
                for j in range(GC):
                    c = g * GC + j
                    m = do("vector", lambda e, c=c, j=j, bank=bank: e.scalar_tensor_tensor(
                        junk[c % (2 * GC)], iota_f[0:PE_P, 0:NB], bkf[:, c:c + 1], bank[0:PE_P, j * NB:(j + 1) * NB],
                        ALU.is_equal, ALU.mult, accum_out=posf[:, c:c + 1]), m_rk[g], m_rec,
                        *([m_sel[g - 2]] if g >= 2 else []), inc="sel" if j == GC - 1 else None)
                m_sel[g] = m
            for g in range(i * SG // GC, (i + 1) * SG // GC):
                select(g)
            c0 = i * SG
            A, Bb, C = posS[:, 0:SG], posS[:, SG:2 * SG], posS[:, 2 * SG:3 * SG]
            m = do("vector", lambda e, c0=c0: e.tensor_copy(A, posf[:, c0:c0 + SG]), m_sel[(i + 1) * SG // GC - 1], inc="slot")
            do("vector", lambda e: e.tensor_single_scalar(Bb, A, 127, op=ALU.bitwise_and), m, inc="slot")
            m = do("vector", lambda e: e.tensor_single_scalar(C, A, 7, op=ALU.logical_shift_right), m, inc="slot")
            m = do("vector", lambda e, c0=c0: e.scalar_tensor_tensor(
                posI[:, c0:c0 + SG], Bb, float(NCOL), C, ALU.mult, ALU.add), m, inc="slot")
            for c in range(c0, c0 + SG):
                m_scat = do("gpsimd", lambda e, c=c: e.indirect_dma_start(
                    tabd, bass.IndirectOffsetOnAxis(ap=posI[:, c:c + 1], axis=0), rec[:, 4 * c:4 * c + 4], None),
                    m, m_fill, inc=f"scat{c % 8}", by=16)
        scat_all = [(f"scat{k}", Q.count[f"scat{k}"]) for k in range(8)]
        half = NCOL // 2
        ci = bkf[0:NB, 0:half].bitcast(I32)
        ge = Bt[0][0:NB, 0:half]
        for k in range(2):
            mi = do("gpsimd", lambda e, k=k: e.iota(ci, pattern=[[1, half]], base=k * half, channel_multiplier=0),
                    m_sel[NG - 1], *([("bmap", 1)] if k else []), inc="iotac")
            mm = do("vector", lambda e: e.tensor_scalar(ge, ci, s_sc, None, ALU.is_ge),
                    mi, m_rk[NG - 1], *([("bmap_p", 1)] if k else []), inc="bmap")
            for h in range(2):
                pm = do("tensor", lambda e, h=h: e.matmul(psum[2 + h][0:1, 0:440], onesb[0:NB, 0:1], ge[:, h * 440:(h + 1) * 440],
                        start=True, stop=True), mm, *([("bmap", 2)] if k else []), inc="bmap_p" if h else None)
            for h in range(2):
                at = k * half + h * 440
                m_bk = do("vector", lambda e, h=h, at=at: e.tensor_scalar(
                    bkI[0:1, at:at + 440], psum[2 + h][0:1, 0:440], -1.0, float(F), ALU.add, ALU.mult), pm,
                    inc="bmap" if h else None)

        free = [[] for _ in range(8)]
        turn = [0]

        def take(lo=0, hi=8):
            i = lo + turn[0] % (hi - lo)
            turn[0] += 1
            return i

        m_W1 = dma("sync", W1s[:, :, :], W1.rearrange("(k p) f -> p k f", p=P), inc="ld_W1")
        m_W2 = dma("sync", W2s[:, :, :], W2.rearrange("(k p) f -> p k f", p=P), inc="ld_W2")
        rows = pre[:, :]
        dma("sync", rows[0:2, :], gamma.rearrange("(m p) -> m p", p=P), inc="ld_pre")
        dma("sync", rows[2:4, :], beta.rearrange("(m p) -> m p", p=P), inc="ld_pre")
        dma("sync", rows[4:20, :], b1.rearrange("e (m p) -> (e m) p", p=P), inc="ld_pre")
        m = dma("sync", rows[20:36, :], rw.rearrange("e (k p) -> (e k) p", p=P), inc="ld_pre")
        m_b2 = dma("sync", b2s[:, :], b2, inc="ld_b2")
        m = do("tensor", lambda e: e.transpose(psum[0][:, 0:36], rows, ident[0:36, 0:36]), m, m_ident, m_gb, inc="pre_t")
        do("vector", lambda e: e.tensor_copy(gbT[:, :], psum[0][:, 0:4]), m, inc="pre_c")
        do("vector", lambda e: e.tensor_copy(b1T[:, :, :].rearrange("p e m -> p (e m)"), psum[0][:, 4:20]), inc="pre_c")
        m_pre = do("vector", lambda e: e.tensor_copy(
            rwT[:, :, :], psum[0][:, 20:36].rearrange("p (e k) -> p k e", k=2)), inc="pre_c")
        m_gbT = m_b1 = m_rw = m_pre

        m_tab = dma("sync", tab, tab_rows, *scat_all, m_bk, inc="ld_tab")

        def aggregate(t, hd, *ready):
            mg, ms, mm, ma = {}, {}, {}, {}
            wait("gpsimd", m_tab, *ready)
            wait("vector", m_tab, *ready)
            regs = {}

            def load(c):
                n = min(RL, CH - c)

                def go(e):
                    _, v = nc.values_load_multi_w_load_instructions(
                        bkI[0:1, c:c + n], engines=[e.engine], min_val=0, max_val=(NB - 1) * F,
                        skip_runtime_bounds_check_because="a count of blocks, 1 to NB, less one, times F")
                    for k in range(n):
                        regs[c + k] = v[k]
                Q.q["vector"].append(go)

            def add(c):
                if c % RL == 0:
                    load(c)

                def go(e):
                    a = acc[:, bass.ds(regs[c], F)]
                    return e.tensor_tensor(a, psum[c % PR][:, 0:F], a, ALU.add)
                ma[c] = do("vector", go, mm[c], *([ma[c - 1]] if c else []), inc=f"{t}_add")

            LAG = 4
            for c in range(CH + LAG):
                if c < CH:
                    prev = [mm[c - GR]] if c >= GR else []
                    mg[c] = do("gpsimd", lambda e, c=c: e.indirect_dma_start(
                        G[c % GR], None, hd, bass.IndirectOffsetOnAxis(ap=tab3[:, c, 0:1].bitcast(I32), axis=0)),
                        *prev, inc=f"gat{c % GR}", by=16)
                    prev = [mm[c - SR]] if c >= SR else []
                    ms[c] = do("vector", lambda e, c=c: e.tensor_scalar(
                        S[c % SR], iota_f[:, :], tab3[:, c, 1:2], tab3[:, c, 2:3], ALU.is_equal, ALU.mult),
                        *prev, inc=f"{t}_sel")
                    prev = [ma[c - PR]] if c >= PR else free[c % PR]
                    mm[c] = do("tensor", lambda e, c=c: e.matmul(psum[c % PR][:, 0:F], S[c % SR], G[c % GR], start=True, stop=True),
                               mg[c], ms[c], *prev, inc=f"{t}_mm")
                if c >= LAG:
                    add(c - LAG)
            for k in range(8):
                free[k] = [ma[CH - 1]]
            return mm[CH - 1], ma[CH - 1]

        def transposes(src_cols, nblk, marks, name):
            ks = []
            for k in range(2):
                i = take()
                for j in range(nblk):
                    m = do("tensor", lambda e, i=i, j=j, k=k: e.transpose(
                        psum[i][:, j * P:(j + 1) * P], src_cols(j, k), ident[:, :]), *marks, *free[i],
                        inc=name if j == nblk - 1 else None)
                ks.append((i, m))
            return ks

        def copy_out(eng, ks, dst, nblk, name, marks):
            for k, (i, m) in enumerate(ks):
                o = dst[:, k * 512:k * 512 + nblk * P]
                if eng == "scalar":
                    c = do(eng, lambda e, i=i, o=o: e.activation(o, psum[i][:, 0:nblk * P], ACT.Copy), m, *marks, inc=name)
                else:
                    c = do(eng, lambda e, i=i, o=o: e.tensor_copy(o, psum[i][:, 0:nblk * P]), m, *marks, inc=name)
                free[i] = [c]
            return c

        sums = small[:, 240:340]
        sqs = small[:, 340:440]
        bn = small[:, 440:480]

        def dense1(m_agg):
            m_y, a_free, m_tr = {}, {}, {}
            for i, (b0, n) in enumerate(SBS):
                ks = transposes(lambda j, k, b0=b0: acc[:, (b0 + j) * F + k * P:(b0 + j) * F + (k + 1) * P], n, [m_agg, m_ident], "d1_tr")
                mc = copy_out("vector", ks, aT[i % 2], n, "d1_cp", a_free.get(i - 2, []))
                for m_ in range(2):
                    q = take()
                    for k in range(2):
                        m = do("tensor", lambda e, q=q, m_=m_, k=k, i=i, n=n: e.matmul(
                            psum[q][:, 0:n * P], W1s[:, k, m_ * P:(m_ + 1) * P], aT[i % 2][:, k * 512:k * 512 + n * P],
                            start=k == 0, stop=k == 1), mc, m_W1, *free[q], inc="d1_mm" if k else None)
                    a_free[i] = [m]
                    yv = acc[:, b0 * F + m_ * n * P:b0 * F + (m_ + 1) * n * P]
                    m_y[i] = do("scalar", lambda e, q=q, n=n, yv=yv, col=2 * i + m_: e.activation(
                        yv, psum[q][:, 0:n * P], ACT.Copy, accum_out=sums[:, col:col + 1]), m, inc="d1_y")
                    free[q] = [m_y[i]]
            m = m_y[len(SBS) - 1]
            ns = len(SBS)
            for m_ in range(2):
                mr = do("vector", lambda e, m_=m_: e.tensor_reduce(
                    bn[:, m_:m_ + 1], sums[:, 0:2 * ns].rearrange("p (s m) -> p m s", m=2)[:, m_:m_ + 1, :], AX.X, ALU.add), m, inc="bn")
            m = do("vector", lambda e: e.tensor_scalar(bn[:, 2:4], bn[:, 0:2], -1.0 / N, None, ALU.mult), mr, inc="bn")
            for i, (b0, n) in enumerate(SBS):
                for m_ in range(2):
                    nv = n * P if i < ns - 1 else (n - 1) * P + LAST
                    yv = acc[:, b0 * F + m_ * n * P:b0 * F + m_ * n * P + nv]
                    msq = do("scalar", lambda e, m_=m_, nv=nv, yv=yv, col=2 * i + m_: e.activation(
                        sq[col % 2][:, 0:nv], yv, ACT.Square, bias=bn[:, 2 + m_:3 + m_], accum_out=sqs[:, col:col + 1]),
                        m, *([("bn_sq", 2 * i + m_ - 1)] if 2 * i + m_ > 1 else []), inc="bn_sq")
            for m_ in range(2):
                mr = do("vector", lambda e, m_=m_: e.tensor_reduce(
                    bn[:, 4 + m_:5 + m_], sqs[:, 0:2 * ns].rearrange("p (s m) -> p m s", m=2)[:, m_:m_ + 1, :], AX.X, ALU.add), msq, inc="bn")
            m = do("vector", lambda e: e.tensor_scalar(bn[:, 6:8], bn[:, 4:6], 1.0 / N, EPS, ALU.mult, ALU.add), mr, inc="bn")
            m = do("scalar", lambda e: e.activation(bn[:, 8:10], bn[:, 6:8], ACT.Sqrt), m, inc="bn_rt")
            m = do("vector", lambda e: e.reciprocal(bn[:, 10:12], bn[:, 8:10]), m, inc="bn")
            m = do("vector", lambda e: e.tensor_tensor(bn[:, 12:14], bn[:, 10:12], gbT[:, 0:2], ALU.mult), m, m_gbT, inc="bn")
            m = do("vector", lambda e: e.tensor_tensor(bn[:, 14:16], bn[:, 12:14], bn[:, 2:4], ALU.mult), m, inc="bn")
            m_bn = do("vector", lambda e: e.tensor_tensor(bn[:, 16:18], bn[:, 14:16], gbT[:, 2:4], ALU.add), m, inc="bn")
            t_free = {}
            for i, (b0, n) in enumerate(SBS):
                for m_ in range(2):
                    yv = acc[:, b0 * F + m_ * n * P:b0 * F + (m_ + 1) * n * P]
                    mr = do("scalar", lambda e, m_=m_, yv=yv, i=i, n=n: e.activation(
                        aT[i % 2][:, m_ * 512:m_ * 512 + n * P], yv, ACT.Relu, bias=bn[:, 16 + m_:17 + m_], scale=bn[:, 12 + m_:13 + m_]),
                        m_bn, *a_free[len(SBS) - 1], *t_free.get(i - 2, []), inc="d1_h")
                for h in range(0, n, 2):
                    q = take()
                    for j in range(h, h + 2):
                        for m_ in range(2):
                            at = (j - h) * F + m_ * P
                            m = do("tensor", lambda e, q=q, at=at, i=i, m_=m_, j=j: e.transpose(
                                psum[q][:, at:at + P], aT[i % 2][:, m_ * 512 + j * P:m_ * 512 + (j + 1) * P], ident[:, :]),
                                mr, *free[q], inc="d1_bt" if (j > h and m_) else None)
                    t_free[i] = [m]
                    mh = do("vector", lambda e, q=q, b=b0 + h: e.tensor_copy(acc_b(b, 2), psum[q][:, :]), m, mr, inc="d1_hc")
                    free[q] = [mh]
                nf = n if i < ns - 1 else n - 1
                dma("sync", h2[b0 * P:(b0 + nf) * P, :].rearrange("(b p) f -> p b f", p=P),
                    acc_b(b0, nf).rearrange("p (b f) -> p b f", f=F), mh, inc="st_h2")
                if nf < n:
                    m_h2 = dma("sync", h2[(NB - 1) * P:N, :], acc[0:LAST, (NB - 1) * F:NB * F], mh, inc="st_h2")
            return m_h2, mh

        def load_experts(*marks):
            dma("sync", w1s, w1.rearrange("e (k p) f -> p e k f", p=P), *marks, inc="ld_ex")
            return dma("sync", w2s, w2.rearrange("e (k p) f -> p e k f", p=P), inc="ld_ex")

        fr = {}

        def stage_a(i, m_agg):
            b0, n = SBS[i]
            last = i == len(SBS) - 1
            X, T, TT, C = xt[i % 2], tt[0], tT[i % 2], comb[i % 2]
            nf = n - 1 if last else n
            mx = dma("sync", X[:, 0:nf * F].rearrange("p (b f) -> p b f", f=F),
                     x[b0 * P:(b0 + nf) * P, :].rearrange("(b p) f -> p b f", p=P),
                     *m_agg, *fr.get(f"x{i % 2}", []), inc=f"ld_xt{i % 2}")
            if last:
                mz = do("vector", lambda e: e.memset(X[:, nf * F:n * F], 0.0), *fr.get(f"x{i % 2}", []), inc="xz")
                mx = dma("sync", X[0:LAST, nf * F:n * F], x[(NB - 1) * P:N, :], mz, inc=f"ld_xt{i % 2}")
            ks = transposes(lambda j, k: acc[:, (b0 + j) * F + k * P:(b0 + j) * F + (k + 1) * P], n, [*m_agg, m_ident], "d2_tr")
            m_tr = ks[-1][1]
            mc = copy_out("scalar", ks, zT[0], n, "d2_cp", fr.get("zT", []))
            yield
            for h in range(0, n, 2):
                q = take()
                for j in range(h, h + 2):
                    for k in range(2):
                        m = do("tensor", lambda e, q=q, j=j, h=h, k=k: e.matmul(
                            psum[q][:, (j - h) * F:(j - h + 1) * F], zT[0][:, k * 512 + j * P:k * 512 + (j + 1) * P], W2s[:, k, :],
                            start=k == 0, stop=k == 1), mc, m_W2, *free[q], inc="d2_z" if (j > h and k) else None)
                fr["zT"] = [m]
                mx1 = do("vector", lambda e, q=q, h=h: e.tensor_tensor(
                    X[:, h * F:(h + 2) * F], X[:, h * F:(h + 2) * F], psum[q][:, :], ALU.add), m, mx, inc="d2_x1")
                free[q] = [mx1]
            yield
            st = stats[:, 0:24]
            v = small[:, 480:504]
            for j in range(n):
                m = do("vector", lambda e, j=j: e.bn_stats(stats[:, 6 * j:6 * j + 6], X[:, j * F:(j + 1) * F]), mx1,
                       *fr.get("st", []), inc="d2_st")
            for j in range(n):
                m1 = do("vector", lambda e, j=j: e.bn_aggr(v[:, 2 * j:2 * j + 2], stats[:, 6 * j:6 * j + 6]), m, *fr.get("v", []), inc="d2_ag")
            fr["st"] = [m1]
            v3 = v[:, 0:8].rearrange("p (b k) -> p b k", k=2)
            m = do("vector", lambda e: e.tensor_scalar(v[:, 8:8 + n], v3[:, 0:n, 1], EPS, None, ALU.add), m1, inc="d2_ve")
            m = do("scalar", lambda e: e.activation(v[:, 12:12 + n], v[:, 8:8 + n], ACT.Sqrt), m, inc="d2_sq")
            m = do("vector", lambda e: e.reciprocal(v[:, 16:16 + n], v[:, 12:12 + n]), m, inc="d2_rs")
            for j in range(n):
                mt = do("vector", lambda e, j=j: e.tensor_scalar(
                    T[:, j * F:(j + 1) * F], X[:, j * F:(j + 1) * F], v[:, 2 * j:2 * j + 1], v[:, 16 + j:17 + j],
                    ALU.subtract, ALU.mult), m, *fr.get("T", []), inc="d2_t")
            fr["v"] = [mt]
            mo = do("vector", lambda e: e.tensor_tensor(acc_b(b0, n), X[:, 0:n * F], T[:, 0:n * F], ALU.add), mt, m_tr, inc="d2_o")
            fr[f"x{i % 2}"] = [mo]
            yield
            ks = transposes(lambda j, k: T[:, j * F + k * P:j * F + (k + 1) * P], n, [mt], "d2_tt")
            fr["T"] = [ks[-1][1], mo]
            mtT = copy_out("scalar", ks, TT, n, "d2_tc", fr.get(f"tT{i % 2}", []))
            yield
            q = take()
            for j in range(n):
                for k in range(2):
                    m = do("tensor", lambda e, q=q, j=j, k=k: e.matmul(
                        psum[q][:, j * 8:j * 8 + 8], TT[:, k * 512 + j * P:k * 512 + (j + 1) * P], rwT[:, k, :],
                        start=k == 0, stop=k == 1), mtT, m_rw, *free[q], inc="d2_lg" if (j == n - 1 and k) else None)
            L = psum[q][:, 0:8 * n].rearrange("p (b e) -> p b e", e=8)

            def r(at, w=1):
                return rt[:, at:at + n * w] if w == 1 else rt[:, at:at + n * w].rearrange("p (b e) -> p b e", e=w)

            def wide(a):
                return a.rearrange("p (b o) -> p b o", o=1).broadcast_to([P, n, 8])
            p8, m8 = r(8, 8), r(48, 8)
            ix, ixf = rt[:, 88:88 + 8 * n].bitcast(U32), r(128, 8)
            m = do("vector", lambda e: e.tensor_reduce(r(0), L, AX.X, ALU.max), m, *fr.get("rt", []), inc="rt")
            m = do("vector", lambda e: e.tensor_tensor(p8, L, wide(r(0)), ALU.subtract), m, inc="rt")
            free[q] = [m]
            m = do("scalar", lambda e: e.activation(p8, p8, ACT.Exp), m, inc="rt_e")
            m = do("vector", lambda e: e.tensor_reduce(r(0), p8, AX.X, ALU.add), m, inc="rt")
            m = do("vector", lambda e: e.reciprocal(r(4), r(0)), m, inc="rt")
            m = do("vector", lambda e: e.tensor_tensor(p8, p8, wide(r(4)), ALU.mult), m, inc="rt")
            for j in range(n):
                m1 = do("vector", lambda e, j=j: e.max(m8[:, j, :], p8[:, j, :]), m, inc="rt")
            for j in range(n):
                m = do("vector", lambda e, j=j: e.max_index(ix[:, 8 * j:8 * j + 8], m8[:, j, :], p8[:, j, :]), m1, inc="rt")
            do("vector", lambda e: e.tensor_copy(rt[:, 128:128 + 8 * n], ix), m, inc="rt")
            m = do("vector", lambda e: e.tensor_tensor(r(0), m8[:, :, 0], m8[:, :, 1], ALU.add), m, inc="rt")
            m = do("vector", lambda e: e.tensor_scalar(r(0), r(0), 1e-12, None, ALU.max), m, inc="rt")
            m = do("vector", lambda e: e.reciprocal(r(4), r(0)), m, inc="rt")
            m = do("vector", lambda e: e.tensor_tensor(m8, m8, wide(r(4)), ALU.mult), m, inc="rt")
            g0, g1 = r(168, 8), r(208, 8)
            for j in range(n):
                do("vector", lambda e, j=j: e.tensor_scalar(g0[:, j, :], iota_f[:, 0:8], ixf[:, j, 0:1], m8[:, j, 0:1],
                                                            ALU.is_equal, ALU.mult), m, inc="rt")
                m1 = do("vector", lambda e, j=j: e.tensor_scalar(g1[:, j, :], iota_f[:, 0:8], ixf[:, j, 1:2], m8[:, j, 1:2],
                                                                 ALU.is_equal, ALU.mult), inc="rt")
            mcb = do("vector", lambda e: e.tensor_tensor(C[:, 0:8 * n].rearrange("p (b e) -> p b e", e=8), g0, g1, ALU.add),
                     m1, *fr.get(f"c{i % 2}", []), inc="rt")
            fr["rt"] = [mcb]
            yield
            q = take()
            for j in range(n):
                m = do("tensor", lambda e, q=q, j=j: e.transpose(psum[q][0:8, j * P:(j + 1) * P], C[:, 8 * j:8 * j + 8], ident[:, :]),
                       mcb, *free[q], inc="d2_ct" if j == n - 1 else None)
            m = do("scalar", lambda e, q=q: e.activation(cT[0][:, 0:n * P], psum[q][0:8, 0:n * P], ACT.Copy), m, *fr.get("cT", []), inc="d2_cc")
            free[q] = [m]
            for h in range(0, n, 2):
                q = take()
                for j in range(h, h + 2):
                    mb = do("tensor", lambda e, q=q, j=j, h=h: e.matmul(
                        psum[q][:, (j - h) * F:(j - h + 1) * F], cT[0][:, j * P:(j + 1) * P], b2s[:, :], start=True, stop=True),
                        m, m_b2, *free[q], inc="d2_b2" if j > h else None)
                mo = do("vector", lambda e, q=q, h=h: e.tensor_tensor(acc_b(b0 + h, 2), acc_b(b0 + h, 2), psum[q][:, :], ALU.add),
                        mb, mo, inc="d2_o2")
                free[q] = [mo]
            fr["cT"] = [mb]
            ready[i] = (mtT, mcb, mo)

        ready = {}

        def dense2(m_agg, m_ex):
            for _ in stage_a(0, m_agg):
                pass
            def experts(i, b0, n):
                mtT, mcb, mo = ready[i]
                nxt = stage_a(i + 1, m_agg) if i + 1 < len(SBS) else iter(())
                up = {}

                def layer1(ex):
                    H = hT[ex % 2]
                    for m_ in range(2):
                        q = take()
                        for k in range(2):
                            m = do("tensor", lambda e, q=q, k=k, m_=m_: e.matmul(
                                psum[q][:, 0:n * P], w1s[:, ex, k, m_ * P:(m_ + 1) * P], tT[i % 2][:, k * 512:k * 512 + n * P],
                                start=k == 0, stop=k == 1), mtT, m_ex, *free[q], inc="l1" if k else None)
                        fr[f"tT{i % 2}"] = [m]
                        mg = do("scalar", lambda e, q=q, m_=m_: e.activation(
                            H[:, m_ * 512:m_ * 512 + n * P], psum[q][:, 0:n * P], ACT.Gelu, bias=b1T[:, ex, m_:m_ + 1]),
                            m, m_b1, *fr.get(f"hT{ex % 2}", []), inc="gelu")
                        free[q] = [mg]
                    up[ex] = mg

                def layer2(ex):
                    H = hT[ex % 2]
                    nonlocal mo
                    new = None
                    for h in range(0, n, 2):
                        q = take()
                        for j in range(h, h + 2):
                            for k in range(2):
                                m = do("tensor", lambda e, q=q, j=j, h=h, k=k: e.matmul(
                                    psum[q][:, (j - h) * F:(j - h + 1) * F], H[:, k * 512 + j * P:k * 512 + (j + 1) * P],
                                    w2s[:, ex, k, :], start=k == 0, stop=k == 1), up[ex], *free[q],
                                    inc="l2" if (j > h and k) else None)
                        fr[f"hT{ex % 2}"] = [m]
                        for j in range(h, h + 2):
                            a = acc_b(b0 + j)
                            new = do("vector", lambda e, q=q, j=j, h=h, a=a: e.scalar_tensor_tensor(
                                a, psum[q][:, (j - h) * F:(j - h + 1) * F], comb[i % 2][:, 8 * j + ex:8 * j + ex + 1], a,
                                ALU.mult, ALU.add), m, mo, mcb, inc="moe")
                        free[q] = [new]
                    mo = new

                layer1(0)
                for ex in range(NEXP):
                    if ex + 1 < NEXP:
                        layer1(ex + 1)
                    next(nxt, None)
                    layer2(ex)
                for _ in nxt:
                    pass
                fr[f"c{i % 2}"] = [mo]
                nf = n - 1 if i == len(SBS) - 1 else n
                mso = dma("sync", out[b0 * P:(b0 + nf) * P, :].rearrange("(b p) f -> p b f", p=P),
                          acc_b(b0, nf).rearrange("p (b f) -> p b f", f=F), mo, inc="st_out")
                if nf < n:
                    mso = dma("sync", out[(NB - 1) * P:N, :], acc[0:LAST, (NB - 1) * F:NB * F], mo, inc="st_out")
                return mso

            for i, (b0, n) in enumerate(SBS):
                mso = experts(i, b0, n)
            return mso

        m_h1 = ("st_h1", Q.count["st_h1"])
        free[0] = free[1] = [m_bk, m_pre]
        for k in range(2, 8):
            free[k] = [m_bk]
        pe1, agg1 = aggregate("a1", h1, m_h1, m_bk)
        m_h2, m_hc = dense1(agg1)
        pe2, agg2 = aggregate("a2", h2, m_h2, m_hc)
        m_ex = load_experts(pe2, agg2)
        last = dense2([agg2], m_ex)
        wait("sync", last)

        block = ctx.enter_context(nc.Block())
        Q.run(block)


_INS = ["x", "src", "dst", "edge_weight", "L0_gnn_W1", "L0_gnn_W2", "L0_gnn_gamma", "L0_gnn_beta",
        "L0_ffn_router_w", "L0_ffn_w1", "L0_ffn_b1", "L0_ffn_w2", "L0_ffn_b2"]


def kernel(**inputs):
    import numpy as np
    import concourse.bacc as bacc
    from concourse.bass_utils import run_bass_kernel_spmd

    nc = bacc.Bacc("TRN2", target_bir_lowering=False, num_devices=1)
    arrays, args = {}, []
    for name in _INS:
        a = np.ascontiguousarray(inputs[name])
        arrays[f"in_{name}"] = a
        args.append(nc.dram_tensor(f"in_{name}", a.shape, mybir.dt.from_np(a.dtype), kind="ExternalInput").ap())
    out = nc.dram_tensor("out_0", (N, F), F32, kind="ExternalOutput").ap()
    build(nc, *args, out)
    r = run_bass_kernel_spmd(nc, [arrays], core_ids=[0])
    return r.results[0]["out_0"]
```

```python
import concourse.bass as bass
from concourse import mybir
from contextlib import ExitStack

F32 = mybir.dt.float32
BF16 = mybir.dt.bfloat16
I32 = mybir.dt.int32
U32 = mybir.dt.uint32
ALU = mybir.AluOpType
ACT = mybir.ActivationFunctionType
AX = mybir.AxisListType

N = 12500
F = 256
E = 212500
P = 128
NB = 98
LAST = N - (NB - 1) * P
PE_P = 125
EC = 1700
GC = 5
NG = EC // GC
GE = GC * PE_P
TG, PG = 4, 85
SG = 20
NSG = EC // SG
KC = 19
NCF = NB * KC
KLO = 15
KLO_LAST = 9
RW = F + 4
CH = (E + NB * 127) // 128
NCOL = 1760
XB = 14
NX = 7
SB = 4
SBS = [(b, min(SB, NB - b)) for b in range(0, NB, SB)]
NEXP = 8
EPS = 1e-05
PR = 8
MR = 4
RL = 8


class Queues:

    def __init__(self, nc, ctx):
        self.nc, self.ctx = nc, ctx
        self.sems, self.count, self.passed = {}, {}, {}
        self.q = self.fresh()

    def fresh(self):
        return {"sync": [], "scalar": [], "vector": [], "tensor": [], "gpsimd": []}

    def sem(self, name):
        if name not in self.sems:
            self.sems[name] = self.ctx.enter_context(self.nc.semaphore(name))
        return self.sems[name]

    def wait(self, eng, *marks):
        for name, value in marks:
            if self.passed.get((eng, name), 0) < value:
                self.passed[(eng, name)] = value
                s = self.sem(name)
                self.q[eng].append(lambda e, s=s, value=value: e.wait_ge(s, value))

    def do(self, eng, fn, *marks, inc=None, by=1):
        self.wait(eng, *marks)
        if inc is None:
            self.q[eng].append(fn)
            return None
        s = self.sem(inc)
        self.count[inc] = self.count.get(inc, 0) + by
        self.q[eng].append(lambda e, s=s: fn(e).then_inc(s, by))
        return inc, self.count[inc]

    def dma(self, eng, out, in_, *marks, inc):
        return self.do(eng, lambda e: e.dma_start(out, in_), *marks, inc=inc, by=16)

    def path(self, make):
        kept = self.q, dict(self.count), dict(self.passed)
        self.q = self.fresh()
        make()
        made = self.q
        self.q, self.count, self.passed = kept
        return made

    def run(self, block, nc, flag, m_flag, fast, slow):
        for name in self.q:
            self.wait(name, m_flag)
            {"sync": block.sync, "scalar": block.scalar, "vector": block.vector,
             "tensor": block.tensor, "gpsimd": block.gpsimd}[name](
                lambda eng, name=name: self.body(eng, nc, name, flag, fast, slow))

    def body(self, eng, nc, name, flag, fast, slow):
        for fn in self.q[name]:
            fn(eng)
        v = nc.values_load(flag, engines=[eng.engine], min_val=0, max_val=1,
                           skip_runtime_bounds_check_because="a minimum with 1 of a count")
        with eng.If(v == 0):
            for fn in fast[name]:
                fn(eng)
        with eng.Else():
            for fn in slow[name]:
                fn(eng)


def build(nc, x, src, dst, ew, W1, W2, gamma, beta, rw, w1, b1, w2, b2, out, force=None):
    h1 = nc.dram_tensor("h1", (N, F), F32, kind="Internal").ap()
    h2 = nc.dram_tensor("h2", (N, F), F32, kind="Internal").ap()
    tabd = nc.dram_tensor("tabd", (P * NCOL, 4), F32, kind="Internal").ap()
    tab_rows = tabd.rearrange("(p c) k -> p (c k)", p=P)
    msgd = nc.dram_tensor("msgd", (P * NCF, RW), F32, kind="Internal").ap()
    msg3 = msgd.rearrange("(p c) k -> p c k", p=P)
    offd = nc.dram_tensor("offd", (1, E), BF16, kind="Internal").ap()

    with ExitStack() as ctx:
        Q = Queues(nc, ctx)
        do, dma, wait = Q.do, Q.dma, Q.wait

        def sb(name, shape, dt=F32):
            return ctx.enter_context(nc.sbuf_tensor(name, shape, dt))

        TOP = 48900
        M = sb("M", [P, TOP])
        ident = sb("ident", [P, P])
        iota_f = sb("iota_f", [P, P])
        iota_p = sb("iota_p", [P, 1])
        W1s = sb("W1s", [P, 2, F])
        W2s = sb("W2s", [P, 2, F])
        gbT = sb("gbT", [P, 4])
        rwT = sb("rwT", [P, 2, NEXP])
        b1T = sb("b1T", [P, NEXP, 2])
        b2s = sb("b2s", [NEXP, F])
        pre = sb("pre", [36, P])
        bkI = sb("bkI", [1, NCOL], I32)
        small = sb("small", [P, 640])
        psum = [ctx.enter_context(nc.psum_tensor(f"ps{i}", [P, 512], F32)) for i in range(8)]

        class Cut:

            def __init__(self, at, end=TOP):
                self.at, self.end = at, end

            def __call__(self, n, p=P):
                a = self.at
                self.at += n
                assert self.at <= self.end, (self.at, self.end)
                return M[0:p, a:a + n]

        acc = M[:, 0:NB * F]
        R0 = NB * F
        cut = Cut(R0)
        bkf = cut(EC, PE_P)
        rec = cut(EC * 4, PE_P)
        rec3 = rec.rearrange("p (c k) -> p c k", k=4)
        ones = cut(P)
        lowT = cut(P)
        onesb = cut(P // 2).bitcast(BF16)
        lowb = cut(P // 2).bitcast(BF16)
        cum = cut(NG, NB)
        gb = cut(NG, NB)
        zrow = cut(1040)
        raw0 = cut.at
        NBB = 3
        Bt = [cut(SG * NB // 2, PE_P).bitcast(BF16) for i in range(NBB)]
        NDG = 4
        dg = [cut(NB, NB) for i in range(NDG)]
        junk = [cut(NB, PE_P) for i in range(2 * GC)]
        WR = 3
        Win = [cut(F) for i in range(WR)]
        offb = [cut((GE + 1) // 2).bitcast(BF16)[:, 0:GE] for i in range(WR)]
        OH = [cut(GE) for i in range(2)]
        msg = [cut(GC * RW, PE_P) for i in range(MR)]
        raw = Cut(raw0, TOP)
        rS, rB, rD, rW = raw(TG * GE, PG), raw(TG * GE, PG), raw(TG * GE, PG), raw(TG * GE, PG)
        offs = raw(TG * GE // 2, PG).bitcast(BF16)
        offm = rec[0:PG, 0:TG * GE]
        s_tot = small[0:NB, 0:1]
        s_nI = small[0:NB, 1:2].bitcast(I32)
        s_n = small[0:NB, 2:3]
        s_sc = small[0:NB, 3:4]
        s_lo = small[0:NB, 4:5]
        s_sc128 = small[0:NB, 5:6]
        r0f = small[0:PG, 8:8 + TG]
        r0I = small[0:TG, 16:16 + PG].bitcast(I32)
        viol = small[:, 104:108]
        flagI = small[0:1, 110:111].bitcast(I32)
        posf = small[0:PE_P, 112:112 + MR * GC]
        posA = small[0:PE_P, 136:136 + 3 * GC].bitcast(I32)
        posI = small[0:PE_P, 152:152 + MR * GC].bitcast(I32)
        stats = small[:, 176:176 + XB * 6]
        mv = small[:, 264:264 + XB * 2]
        nrm = small[:, 296:296 + XB * 2]

        def acc_b(b, n=1):
            return acc[:, b * F:(b + n) * F]

        free = [[] for _ in range(8)]
        turn = [0, 0, 8]

        def take():
            i = turn[1] + turn[0] % (turn[2] - turn[1])
            turn[0] += 1
            return i

        m = do("gpsimd", lambda e: e.iota(iota_f[:, :].bitcast(I32), pattern=[[1, P]], base=0, channel_multiplier=0), inc="iota")
        m_iota = do("vector", lambda e: e.tensor_copy(iota_f[:, :], iota_f[:, :].bitcast(I32)), m, inc="iotaf")
        m = do("gpsimd", lambda e: e.iota(iota_p[:, :].bitcast(I32), pattern=[[0, 1]], base=0, channel_multiplier=1), inc="iota")
        m_iotap = do("vector", lambda e: e.tensor_copy(iota_p[:, :], iota_p[:, :].bitcast(I32)), m, inc="iotaf")
        do("gpsimd", lambda e: e.memset(ident[:, :], 0.0), inc="cst")
        m2 = do("gpsimd", lambda e: e.memset(ones, 1.0), inc="cst")
        m_ident = do("gpsimd", lambda e: e.affine_select(out=ident[:, :], in_=ident[:, :], compare_op=ALU.not_equal, fill=1.0,
                     base=0, pattern=[[-1, P]], channel_multiplier=1), m2, inc="cst")
        m_low = do("gpsimd", lambda e: e.affine_select(out=lowT, in_=ones, compare_op=ALU.is_gt, fill=0.0,
                   base=0, pattern=[[1, P]], channel_multiplier=-1), m_ident, inc="cst")
        m_zrow = do("gpsimd", lambda e: e.memset(zrow, 0.0), inc="cst")
        do("vector", lambda e: e.tensor_copy(onesb, ones), m_low, inc="cstb")
        m_cstb = do("vector", lambda e: e.tensor_copy(lowb, lowT), inc="cstb")
        m_vz = do("vector", lambda e: e.memset(viol, 0.0), inc="cstb")

        def run4(a):
            return a.rearrange("(t p k) -> p t k", t=TG, p=PG)

        m_src = dma("sync", rS.bitcast(I32).rearrange("p (t k) -> p t k", t=TG), run4(src), inc="ld_src")
        m_dst = dma("sync", rD.bitcast(I32).rearrange("p (t k) -> p t k", t=TG), run4(dst), inc="ld_dst")
        m_ew = dma("sync", rW.rearrange("p (t k) -> p t k", t=TG), run4(ew), inc="ld_w")

        m_accz = do("gpsimd", lambda e: e.memset(acc_b(NB - 1), 0.0), inc="accz")
        m_x = []
        for i in range(NX):
            b0 = i * XB
            n = XB if i < NX - 1 else XB - 1
            m = dma("scalar", acc_b(b0, n).rearrange("p (b f) -> p b f", f=F),
                    x[b0 * P:(b0 + n) * P, :].rearrange("(b p) f -> p b f", p=P), inc=f"ld_x{i}")
            if i == NX - 1:
                m = dma("scalar", acc[0:LAST, (NB - 1) * F:NB * F], x[(NB - 1) * P:N, :], m_accz, inc=f"ld_x{i}")
            m_x.append(m)

        m3 = msg3[:, 0:(NB - 1) * KC, :].rearrange("p (b k) r -> p b (k r)", k=KC)
        zw = zrow[:, :].rearrange("p (o r) -> p o r", o=1)
        for b in range(0, NB - 1, 14):
            n = min(14, NB - 1 - b)
            dma("sync", m3[:, b:b + n, KLO * RW:KC * RW], zw[:, :, 0:(KC - KLO) * RW].broadcast_to([P, n, (KC - KLO) * RW]), m_zrow, inc="fillm")
        lastm = msg3[:, (NB - 1) * KC:NB * KC, :].rearrange("p k r -> p (k r)")
        for k in range(KLO_LAST, KC, 4):
            n = min(4, KC - k)
            m_fillm = dma("sync", lastm[:, k * RW:(k + n) * RW], zrow[:, 0:n * RW], inc="fillm")
        for k in range(0, NCOL * 4, 1040):
            n = min(1040, NCOL * 4 - k)
            m_fill = dma("sync", tab_rows[:, k:k + n], zrow[:, 0:n], inc="fill")

        rSI, rBI, rDI = rS.bitcast(I32), rB.bitcast(I32), rD.bitcast(I32)
        m = do("vector", lambda e: e.tensor_single_scalar(rBI, rSI, 7, op=ALU.logical_shift_right), m_src, inc="edg")
        m = do("vector", lambda e: e.tensor_single_scalar(rSI, rSI, 127, op=ALU.bitwise_and), m, inc="edg")
        m = do("vector", lambda e: e.tensor_copy(rB, rBI), m, inc="edg")
        m = do("vector", lambda e: e.tensor_copy(rS, rSI), m, inc="edg")
        m = do("vector", lambda e: e.tensor_copy(rD, rDI), m_dst, inc="edg")
        rD3 = rD.rearrange("p (t k) -> p t k", t=TG)
        m_r0 = do("vector", lambda e: e.tensor_scalar(r0f, rD3[:, :, 0], float(N - P), None, ALU.min), m, inc="edg")
        o3, om3 = offs.rearrange("p (t k) -> p t k", t=TG), offm.rearrange("p (t k) -> p t k", t=TG)
        for t in range(TG):
            m = do("vector", lambda e, t=t: e.tensor_scalar(om3[:, t, :], rD3[:, t, :], r0f[:, t:t + 1], None, ALU.subtract), m_r0, inc="edg")
        m_off = do("vector", lambda e: e.tensor_copy(offs, offm), m, inc="edg")
        do("vector", lambda e: e.tensor_reduce(viol[0:PG, 0:1], offm, AX.X, ALU.max), m_vz, inc="viol")
        m = do("vector", lambda e: e.tensor_reduce(viol[0:PG, 1:2], offm, AX.X, ALU.min), inc="viol")
        do("vector", lambda e: e.tensor_scalar(viol[0:PG, 0:1], viol[0:PG, 0:1], float(P - 1), None, ALU.is_gt), m, inc="viol")
        m_v1 = do("vector", lambda e: e.tensor_scalar(viol[0:PG, 1:2], viol[0:PG, 1:2], 0.0, None, ALU.is_lt), inc="viol")
        m_offd = dma("sync", offd.rearrange("o (t p k) -> p (o t) k", t=TG, p=PG), o3, m_off, inc="st_off")
        m = do("tensor", lambda e: e.transpose(psum[7][0:TG, 0:PG], r0f, ident[0:PG, 0:PG]), m_r0, m_ident, inc="r0")
        m_r0I = do("vector", lambda e: e.tensor_copy(r0I, psum[7][0:TG, 0:PG]), m, inc="r0c")
        free[7] = [m_r0I]

        for w, (raw_, mr, to) in enumerate([(rB, m_r0, bkf.rearrange("p (g j) -> p g j", j=GC)),
                                            (rD, m_r0, rec3[:, :, 0].rearrange("p (g j) -> p g j", j=GC)),
                                            (rS, m_r0, rec3[:, :, 1].rearrange("p (g j) -> p g j", j=GC)),
                                            (rW, m_ew, rec3[:, :, 2].rearrange("p (g j) -> p g j", j=GC))]):
            for t in range(TG):
                i = take()
                for j in range(GC):
                    m = do("tensor", lambda e, i=i, j=j, raw_=raw_, t=t: e.transpose(
                        psum[i][0:PE_P, j * PG:(j + 1) * PG], raw_[:, t * GE + j * PE_P:t * GE + (j + 1) * PE_P], ident[0:PG, 0:PG]),
                        mr, m_ident, *free[i], inc="etr" if j == GC - 1 else None)
                m_ec = do("vector", lambda e, i=i, t=t, to=to: e.tensor_copy(
                    to[:, t * PG:(t + 1) * PG, :], psum[i][0:PE_P, 0:GC * PG].rearrange("p (j g) -> p g j", j=GC)),
                    m, m_v1, inc="etc")
                free[i] = [m_ec]
            if w == 0:
                m_bkf = m_ec
        m_rec = do("vector", lambda e: e.memset(rec3[:, :, 3], 0.0), m_v1, inc="etc")

        def norm_group(i):
            b0 = i * XB
            for j in range(XB):
                m = do("vector", lambda e, j=j: e.bn_stats(stats[:, 6 * j:6 * j + 6], acc_b(b0 + j)),
                       m_x[i], *([("ln_ab", i)] if i else []), inc="ln_st")
            for j in range(XB):
                m2 = do("vector", lambda e, j=j: e.bn_aggr(mv[:, 2 * j:2 * j + 2], stats[:, 6 * j:6 * j + 6]), m, inc="ln_ag")
            mv3 = mv.rearrange("p (b k) -> p b k", k=2)
            m = do("vector", lambda e: e.tensor_scalar(nrm[:, 0:XB], mv3[:, :, 1], EPS, None, ALU.add),
                   m2, *([("ln_h", XB * i)] if i else []), inc="ln_ve")
            m = do("scalar", lambda e: e.activation(nrm[:, 0:XB], nrm[:, 0:XB], ACT.Sqrt), m, inc="ln_sq")
            m = do("vector", lambda e: e.reciprocal(nrm[:, 0:XB], nrm[:, 0:XB]), m, inc="ln_rs")
            m = do("vector", lambda e: e.scalar_tensor_tensor(nrm[:, XB:2 * XB], mv3[:, :, 0], -1.0, nrm[:, 0:XB], ALU.mult, ALU.mult),
                   m, inc="ln_ab")
            for j in range(XB):
                mh = do("scalar", lambda e, j=j: e.activation(acc_b(b0 + j), acc_b(b0 + j), ACT.Identity,
                        bias=nrm[:, XB + j:XB + j + 1], scale=nrm[:, j:j + 1]), m, inc="ln_h")
            n = XB if i < NX - 1 else XB - 1
            dma("sync", h1[b0 * P:(b0 + n) * P, :].rearrange("(b p) f -> p b f", p=P),
                acc_b(b0, n).rearrange("p (b f) -> p b f", f=F), mh, inc="st_h1")
            if i == NX - 1:
                dma("sync", h1[(NB - 1) * P:N, :], acc[0:LAST, (NB - 1) * F:NB * F], mh, inc="st_h1")

        def onehot(i, *marks):
            c0 = (i % NSG) * SG
            Bv = Bt[i % NBB].rearrange("p (c b) -> p c b", b=NB)
            return do("vector", lambda e: e.tensor_tensor(
                Bv, bkf[:, c0:c0 + SG].rearrange("p (c o) -> p c o", o=1).broadcast_to([PE_P, SG, NB]),
                iota_f[0:PE_P, 0:NB].rearrange("p (o b) -> p o b", o=1).broadcast_to([PE_P, SG, NB]), ALU.is_equal),
                *marks, inc="oneh")

        i0 = take()
        cnt = psum[i0][0:NB, 0:NG]
        m_cnt = {}
        for i in range(NSG):
            mb = onehot(i, m_ec, m_iota, *([m_cnt[i - NBB]] if i >= NBB else []))
            if i % 12 == 5 and i // 12 < NX:
                norm_group(i // 12)
            for c in range(SG):
                g, j = i * (SG // GC) + c // GC, c % GC
                fn = lambda e, i=i, c=c, g=g, j=j: e.matmul(
                    cnt[:, g:g + 1], Bt[i % NBB][:, c * NB:(c + 1) * NB], onesb[0:PE_P, 0:1], start=j == 0, stop=j == GC - 1)
                m = do("tensor", fn, mb, m_cstb, *free[i0], inc="cnt" if c == SG - 1 else None)
            m_cnt[i] = m
        m_cntz = m
        m = do("vector", lambda e: e.tensor_tensor_scan(cum, ones[0:NB, 0:1].broadcast_to([NB, NG]), cnt, 0.0, ALU.mult, ALU.add), m, inc="base")
        do("vector", lambda e: e.tensor_scalar(s_lo, iota_p[0:NB, :], float(NB - 1), float((KLO_LAST - KLO) * P), ALU.is_equal, ALU.mult), m_iotap, inc="base")
        m_cum = do("vector", lambda e: e.tensor_tensor(gb, cum, cnt, ALU.subtract), m, inc="base")
        free[i0] = [m_cum]
        tot = cum[:, NG - 1:NG]
        do("vector", lambda e: e.tensor_scalar(viol[0:NB, 2:3], tot, float(KC * P), None, ALU.is_gt), m_cum, inc="viol")
        m = do("vector", lambda e: e.tensor_scalar(s_lo, s_lo, float(KLO * P), None, ALU.add), m_cum, inc="viol")
        m = do("vector", lambda e: e.tensor_tensor(viol[0:NB, 3:4], tot, s_lo, ALU.is_lt), m, inc="viol")
        i1 = take()
        m = do("tensor", lambda e: e.matmul(psum[i1][0:1, 0:4], ones[:, 0:1], viol, start=True, stop=True), m, *free[i1], inc="vsum")
        m = do("vector", lambda e: e.tensor_reduce(small[0:1, 109:110], psum[i1][0:1, 0:4], AX.X, ALU.add), m, inc="viol")
        free[i1] = [m]
        if force is not None:
            m = do("vector", lambda e: e.tensor_scalar(small[0:1, 109:110], small[0:1, 109:110], float(force), None, ALU.add), m, inc="viol")
        m_flag = do("vector", lambda e: e.tensor_scalar(flagI, small[0:1, 109:110], 1.0, None, ALU.min), m, inc="viol")

        m_W1 = dma("sync", W1s[:, :, :], W1.rearrange("(k p) f -> p k f", p=P), inc="ld_W1")
        m_W2 = dma("sync", W2s[:, :, :], W2.rearrange("(k p) f -> p k f", p=P), inc="ld_W2")
        rows = pre[:, :]
        dma("sync", rows[0:2, :], gamma.rearrange("(m p) -> m p", p=P), inc="ld_pre")
        dma("sync", rows[2:4, :], beta.rearrange("(m p) -> m p", p=P), inc="ld_pre")
        dma("sync", rows[4:20, :], b1.rearrange("e (m p) -> (e m) p", p=P), inc="ld_pre")
        m = dma("sync", rows[20:36, :], rw.rearrange("e (k p) -> (e k) p", p=P), inc="ld_pre")
        m_b2 = dma("sync", b2s[:, :], b2, inc="ld_b2")
        i2 = take()
        m = do("tensor", lambda e: e.transpose(psum[i2][:, 0:36], rows, ident[0:36, 0:36]), m, m_ident, *free[i2], inc="pre_t")
        do("vector", lambda e: e.tensor_copy(gbT[:, :], psum[i2][:, 0:4]), m, inc="pre_c")
        do("vector", lambda e: e.tensor_copy(b1T[:, :, :].rearrange("p e m -> p (e m)"), psum[i2][:, 4:20]), inc="pre_c")
        m_pre = do("vector", lambda e: e.tensor_copy(
            rwT[:, :, :], psum[i2][:, 20:36].rearrange("p (e k) -> p k e", k=2)), inc="pre_c")
        free[i2] = [m_pre]
        m_gbT = m_b1 = m_rw = m_pre
        m_h1 = ("st_h1", Q.count["st_h1"])

        def scatter(base_marks, ncol, target, m_filled, expand):
            m_rk, m_sel, m_oh, m_ohx, m_scat, m_ev, m_w, m_of = {}, {}, {}, {}, {}, {}, {}, {}
            m_dg, m_B, m_sl = {}, {}, {}
            GS = SG // GC
            if expand:
                for k in range(MR):
                    mz = do("gpsimd", lambda e, k=k: e.memset(msg[k], 0.0), m_offd, m_ec, m_cntz, inc="msgz")

            def load(g):
                old = [m_ohx[g - WR]] if g >= WR else []

                def go(e):
                    t, p_ = divmod(g, PG)
                    _, v = nc.values_load_multi_w_load_instructions(
                        r0I[t:t + 1, p_:p_ + 1], engines=[e.engine], min_val=0, max_val=N - P,
                        skip_runtime_bounds_check_because="a node's number, at most N - P by a minimum")
                    return e.dma_start(Win[g % WR], h1[bass.ds(v[0], P), :])
                m_w[g] = do("sync", go, m_h1, m_r0I, m_offd, m_cntz, m_ec, *old, inc=f"win{g % WR}", by=16)
                m_of[g] = dma("sync", offb[g % WR], offd[:, g * GE:(g + 1) * GE].broadcast_to([P, GE]), *old, inc=f"ofb{g % WR}")

            def rank(g):
                i, c0 = g // GS, (g * GC) % SG
                k = NSG + i
                if g % GS == 0:
                    ob = [m_cnt[k - NBB]] if k - NBB < NSG else [m_rk[(k - NBB - NSG + 1) * GS - 1]]
                    m_B[i] = onehot(k, *base_marks, *ob)
                md = do("vector", lambda e: e.tensor_scalar(dg[g % NDG], ident[0:NB, 0:NB], gb[:, g:g + 1], None, ALU.mult),
                        *base_marks, m_ident, *([m_rk[g - NDG]] if g >= NDG else [m_ec]), inc="diag")
                bank = psum[g % 3][0:PE_P, 0:GC * NB].rearrange("p (c b) -> p c b", b=NB)
                Bv = Bt[k % NBB].rearrange("p (c b) -> p c b", b=NB)
                do("tensor", lambda e: e.matmul(
                    bank, ones[0:NB, 0:PE_P], dg[g % NDG].rearrange("p (o b) -> p o b", o=1).broadcast_to([NB, GC, NB]),
                    start=True, stop=False), md, m_B[i], *([m_sel[g - 3]] if g >= 3 else free[g % 3]))
                for j in range(GC - 1):
                    do("tensor", lambda e, j=j: e.matmul(
                        bank[:, j + 1:GC, :], onesb[0:PE_P, 0:PE_P],
                        Bv[:, c0 + j:c0 + j + 1, :].broadcast_to([PE_P, GC - 1 - j, NB]), start=False, stop=False))
                m_rk[g] = do("tensor", lambda e: e.matmul(
                    bank, lowb[0:PE_P, 0:PE_P], Bv[:, c0:c0 + GC, :], start=False, stop=True), inc="rank")

            def slots(g):
                bank = psum[g % 3]
                r = g % MR
                for j in range(GC):
                    c = g * GC + j
                    m = do("vector", lambda e, c=c, j=j: e.scalar_tensor_tensor(
                        junk[c % (2 * GC)], iota_f[0:PE_P, 0:NB], bkf[:, c:c + 1], bank[0:PE_P, j * NB:(j + 1) * NB],
                        ALU.is_equal, ALU.mult, accum_out=posf[:, r * GC + j:r * GC + j + 1]), m_rk[g], m_rec,
                        *([m_sel[g - 2]] if g >= 2 else []), *([m_sl[g - 1]] if g else []), inc="sel" if j == GC - 1 else None)
                m_sel[g] = m
                A, Bb, C = posA[:, 0:GC], posA[:, GC:2 * GC], posA[:, 2 * GC:3 * GC]
                m = do("vector", lambda e: e.tensor_copy(A, posf[:, r * GC:(r + 1) * GC]), m, inc="slot")
                do("vector", lambda e: e.tensor_single_scalar(Bb, A, 127, op=ALU.bitwise_and), m, inc="slot")
                m = do("vector", lambda e: e.tensor_single_scalar(C, A, 7, op=ALU.logical_shift_right), m, inc="slot")
                m_sl[g] = do("vector", lambda e: e.scalar_tensor_tensor(
                    posI[:, r * GC:(r + 1) * GC], Bb, float(ncol), C, ALU.mult, ALU.add), m,
                    *([m_scat[g - MR]] if g >= MR else []), inc="slot")

            def spread(g):
                m_oh[g] = do("vector", lambda e: e.tensor_scalar(OH[g % 2], offb[g % WR], iota_p[:, :], None, ALU.is_equal),
                             m_of[g], m_iotap, *([m_ohx[g - 2]] if g >= 2 else []), inc="spr")

            def expand_(g):
                r = g % MR
                ev = []
                for h in range(0, GC, 2):
                    i = take()
                    n = min(2, GC - h)
                    for j in range(n):
                        m = do("tensor", lambda e, i=i, j=j, h=h: e.matmul(
                            psum[i][0:PE_P, j * F:(j + 1) * F], OH[g % 2][:, (h + j) * PE_P:(h + j + 1) * PE_P], Win[g % WR],
                            start=True, stop=True), m_oh[g], m_w[g], *free[i], inc="exp" if j == n - 1 else None)
                    ev.append((i, h, n, m))
                m_ohx[g] = m
                M3 = msg[r].rearrange("p (j k) -> p j k", k=RW)
                for i, h, n, m in ev:
                    m_e = do("scalar", lambda e, i=i, h=h, n=n: e.activation(
                        M3[:, h:h + n, 0:F], psum[i][0:PE_P, 0:n * F].rearrange("p (j f) -> p j f", f=F), ACT.Copy),
                        m, mz, *([m_scat[g - MR]] if g >= MR else []), inc="evc")
                    free[i] = [m_e]
                m_ev[g] = do("scalar", lambda e: e.activation(
                    M3[:, :, F:F + 3], rec3[:, g * GC:(g + 1) * GC, 0:3], ACT.Copy), m_rec, inc="evc")

            def send(g):
                r = g % MR
                for j in range(GC):
                    c = g * GC + j
                    row = msg[r][:, j * RW:(j + 1) * RW] if expand else rec[:, 4 * c:4 * c + 4]
                    m_scat[g] = do("gpsimd", lambda e, j=j, row=row: e.indirect_dma_start(
                        target, bass.IndirectOffsetOnAxis(ap=posI[:, r * GC + j:r * GC + j + 1], axis=0), row, None),
                        m_sl[g], m_filled, *([m_ev[g]] if expand else []), inc=f"scat{r}", by=16)

            if expand:
                turn[0], turn[1], turn[2] = 0, 3, 8
                load(0)
                load(1)
                spread(0)
            rank(0)
            rank(1)
            for g in range(NG):
                if g + 2 < NG:
                    rank(g + 2)
                slots(g)
                if expand:
                    if g + 1 < NG:
                        spread(g + 1)
                    expand_(g)
                    if g + 2 < NG:
                        load(g + 2)
                send(g)
            turn[0], turn[1], turn[2] = 0, 0, 8
            for k in range(3):
                free[k] = [m_sel[NG - 1]]
            return [m_scat[NG - 1 - k] for k in range(MR)] + [m_sel[NG - 1], m_sl[NG - 1]], m_rk[NG - 1]

        def transposes(src_cols, nblk, marks, name):
            ks = []
            for k in range(2):
                i = take()
                for j in range(nblk):
                    m = do("tensor", lambda e, i=i, j=j, k=k: e.transpose(
                        psum[i][:, j * P:(j + 1) * P], src_cols(j, k), ident[:, :]), *marks, *free[i],
                        inc=name if j == nblk - 1 else None)
                ks.append((i, m))
            return ks

        def copy_out(eng, ks, dst, nblk, name, marks):
            for k, (i, m) in enumerate(ks):
                o = dst[:, k * 512:k * 512 + nblk * P]
                if eng == "scalar":
                    c = do(eng, lambda e, i=i, o=o: e.activation(o, psum[i][:, 0:nblk * P], ACT.Copy), m, *marks, inc=name)
                else:
                    c = do(eng, lambda e, i=i, o=o: e.tensor_copy(o, psum[i][:, 0:nblk * P]), m, *marks, inc=name)
                free[i] = [c]
            return c

        sums = small[:, 330:430]
        sqs = small[:, 430:530]
        bn = small[:, 530:570]
        ns = len(SBS)

        def dense1_y(i, marks, aT, a_free, cp):
            b0, n = SBS[i]
            ks = transposes(lambda j, k: acc[:, (b0 + j) * F + k * P:(b0 + j) * F + (k + 1) * P], n, [*marks, m_ident], "d1_tr")
            mc = copy_out(cp, ks, aT[i % 2], n, "d1_cp", a_free.get(i - 2, []))
            for m_ in range(2):
                q = take()
                for k in range(2):
                    m = do("tensor", lambda e, q=q, m_=m_, k=k: e.matmul(
                        psum[q][:, 0:n * P], W1s[:, k, m_ * P:(m_ + 1) * P], aT[i % 2][:, k * 512:k * 512 + n * P],
                        start=k == 0, stop=k == 1), mc, m_W1, *free[q], inc="d1_mm" if k else None)
                a_free[i] = [m]
                yv = acc[:, b0 * F + m_ * n * P:b0 * F + (m_ + 1) * n * P]
                my = do("scalar", lambda e, q=q, yv=yv, col=2 * i + m_: e.activation(
                    yv, psum[q][:, 0:n * P], ACT.Copy, accum_out=sums[:, col:col + 1]), m, inc="d1_y")
                free[q] = [my]
            return my

        def dense1_rest(m, aT, sq, a_free):
            for m_ in range(2):
                mr = do("vector", lambda e, m_=m_: e.tensor_reduce(
                    bn[:, m_:m_ + 1], sums[:, 0:2 * ns].rearrange("p (s m) -> p m s", m=2)[:, m_:m_ + 1, :], AX.X, ALU.add), m, inc="bn")
            m = do("vector", lambda e: e.tensor_scalar(bn[:, 2:4], bn[:, 0:2], -1.0 / N, None, ALU.mult), mr, inc="bn")
            for i, (b0, n) in enumerate(SBS):
                for m_ in range(2):
                    nv = n * P if i < ns - 1 else (n - 1) * P + LAST
                    yv = acc[:, b0 * F + m_ * n * P:b0 * F + m_ * n * P + nv]
                    msq = do("scalar", lambda e, m_=m_, nv=nv, yv=yv, col=2 * i + m_: e.activation(
                        sq[col % 2][:, 0:nv], yv, ACT.Square, bias=bn[:, 2 + m_:3 + m_], accum_out=sqs[:, col:col + 1]),
                        m, *([("bn_sq", 2 * i + m_ - 1)] if 2 * i + m_ > 1 else []), inc="bn_sq")
            for m_ in range(2):
                mr = do("vector", lambda e, m_=m_: e.tensor_reduce(
                    bn[:, 4 + m_:5 + m_], sqs[:, 0:2 * ns].rearrange("p (s m) -> p m s", m=2)[:, m_:m_ + 1, :], AX.X, ALU.add), msq, inc="bn")
            m = do("vector", lambda e: e.tensor_scalar(bn[:, 6:8], bn[:, 4:6], 1.0 / N, EPS, ALU.mult, ALU.add), mr, inc="bn")
            m = do("scalar", lambda e: e.activation(bn[:, 8:10], bn[:, 6:8], ACT.Sqrt), m, inc="bn_rt")
            m = do("vector", lambda e: e.reciprocal(bn[:, 10:12], bn[:, 8:10]), m, inc="bn")
            m = do("vector", lambda e: e.tensor_tensor(bn[:, 12:14], bn[:, 10:12], gbT[:, 0:2], ALU.mult), m, m_gbT, inc="bn")
            m = do("vector", lambda e: e.tensor_tensor(bn[:, 14:16], bn[:, 12:14], bn[:, 2:4], ALU.mult), m, inc="bn")
            m_bn = do("vector", lambda e: e.tensor_tensor(bn[:, 16:18], bn[:, 14:16], gbT[:, 2:4], ALU.add), m, inc="bn")
            t_free = {}
            for i, (b0, n) in enumerate(SBS):
                for m_ in range(2):
                    yv = acc[:, b0 * F + m_ * n * P:b0 * F + (m_ + 1) * n * P]
                    mr = do("scalar", lambda e, m_=m_, yv=yv, i=i, n=n: e.activation(
                        aT[i % 2][:, m_ * 512:m_ * 512 + n * P], yv, ACT.Relu, bias=bn[:, 16 + m_:17 + m_], scale=bn[:, 12 + m_:13 + m_]),
                        m_bn, *a_free[ns - 1], *t_free.get(i - 2, []), inc="d1_h")
                for h in range(0, n, 2):
                    q = take()
                    for j in range(h, h + 2):
                        for m_ in range(2):
                            at = (j - h) * F + m_ * P
                            m = do("tensor", lambda e, q=q, at=at, i=i, m_=m_, j=j: e.transpose(
                                psum[q][:, at:at + P], aT[i % 2][:, m_ * 512 + j * P:m_ * 512 + (j + 1) * P], ident[:, :]),
                                mr, *free[q], inc="d1_bt" if (j > h and m_) else None)
                    t_free[i] = [m]
                    mh = do("vector", lambda e, q=q, b=b0 + h: e.tensor_copy(acc_b(b, 2), psum[q][:, :]), m, mr, inc="d1_hc")
                    free[q] = [mh]
                nf = n if i < ns - 1 else n - 1
                dma("sync", h2[b0 * P:(b0 + nf) * P, :].rearrange("(b p) f -> p b f", p=P),
                    acc_b(b0, nf).rearrange("p (b f) -> p b f", f=F), mh, inc="st_h2")
                if nf < n:
                    m_h2 = dma("sync", h2[(NB - 1) * P:N, :], acc[0:LAST, (NB - 1) * F:NB * F], mh, inc="st_h2")
            return m_h2, mh

        class Dense2:

            def __init__(self, cut, Z, tick=None):
                self.Z = Z
                self.w1s = cut(4096).rearrange("p (e k f) -> p e k f", e=NEXP, k=2)
                self.w2s = cut(4096).rearrange("p (e k f) -> p e k f", e=NEXP, k=2)
                self.zT = cut(1024)
                self.xt = [cut(1024) for _ in range(2)]
                self.tt = cut(1024)
                self.tT = [cut(1024) for _ in range(2)]
                self.hT = [cut(1024) for _ in range(2)]
                self.comb = [cut(32) for _ in range(2)]
                self.cT = cut(512, NEXP)
                self.rt = cut(256)
                self.fr, self.ready = {}, {}
                self.tick = tick or (lambda: None)

            def weights(self, *marks):
                dma("sync", self.w1s, w1.rearrange("e (k p) f -> p e k f", p=P), *marks, inc="ld_ex")
                self.m_ex = dma("sync", self.w2s, w2.rearrange("e (k p) f -> p e k f", p=P), inc="ld_ex")

            def first(self, i, m_agg, m_x0):
                fr, Zs, tick = self.fr, self.Z(i), self.tick
                b0, n = SBS[i]
                last = i == ns - 1
                X, T, TT, C, zT, cT, rt = self.xt[i % 2], self.tt, self.tT[i % 2], self.comb[i % 2], self.zT, self.cT, self.rt
                nf = n - 1 if last else n
                mx = dma("sync", X[:, 0:nf * F].rearrange("p (b f) -> p b f", f=F),
                         x[b0 * P:(b0 + nf) * P, :].rearrange("(b p) f -> p b f", p=P),
                         *m_x0, *fr.get(f"x{i % 2}", []), inc=f"ld_xt{i % 2}")
                if last:
                    mz = do("vector", lambda e: e.memset(X[:, nf * F:n * F], 0.0), *m_x0, *fr.get(f"x{i % 2}", []), inc="xz")
                    mx = dma("sync", X[0:LAST, nf * F:n * F], x[(NB - 1) * P:N, :], mz, inc=f"ld_xt{i % 2}")
                ks = transposes(lambda j, k: Zs[:, j * F + k * P:j * F + (k + 1) * P], n, [*m_agg, m_ident], "d2_tr")
                m_tr = ks[-1][1]
                mc = copy_out("scalar", ks, zT, n, "d2_cp", [*m_x0, *fr.get("zT", [])])
                tick()
                yield
                for h in range(0, n, 2):
                    q = take()
                    for j in range(h, h + 2):
                        for k in range(2):
                            m = do("tensor", lambda e, q=q, j=j, h=h, k=k: e.matmul(
                                psum[q][:, (j - h) * F:(j - h + 1) * F], zT[:, k * 512 + j * P:k * 512 + (j + 1) * P], W2s[:, k, :],
                                start=k == 0, stop=k == 1), mc, m_W2, *free[q], inc="d2_z" if (j > h and k) else None)
                    fr["zT"] = [m]
                    mx1 = do("vector", lambda e, q=q, h=h: e.tensor_tensor(
                        X[:, h * F:(h + 2) * F], X[:, h * F:(h + 2) * F], psum[q][:, :], ALU.add), m, mx, inc="d2_x1")
                    free[q] = [mx1]
                    tick()
                yield
                v = small[:, 570:594]
                for j in range(n):
                    m = do("vector", lambda e, j=j: e.bn_stats(stats[:, 6 * j:6 * j + 6], X[:, j * F:(j + 1) * F]), mx1,
                           *fr.get("st", []), inc="d2_st")
                for j in range(n):
                    m1 = do("vector", lambda e, j=j: e.bn_aggr(v[:, 2 * j:2 * j + 2], stats[:, 6 * j:6 * j + 6]), m, *fr.get("v", []), inc="d2_ag")
                fr["st"] = [m1]
                v3 = v[:, 0:8].rearrange("p (b k) -> p b k", k=2)
                m = do("vector", lambda e: e.tensor_scalar(v[:, 8:8 + n], v3[:, 0:n, 1], EPS, None, ALU.add), m1, inc="d2_ve")
                m = do("scalar", lambda e: e.activation(v[:, 12:12 + n], v[:, 8:8 + n], ACT.Sqrt), m, inc="d2_sq")
                m = do("vector", lambda e: e.reciprocal(v[:, 16:16 + n], v[:, 12:12 + n]), m, inc="d2_rs")
                for j in range(n):
                    mt = do("vector", lambda e, j=j: e.tensor_scalar(
                        T[:, j * F:(j + 1) * F], X[:, j * F:(j + 1) * F], v[:, 2 * j:2 * j + 1], v[:, 16 + j:17 + j],
                        ALU.subtract, ALU.mult), m, *m_x0, *fr.get("T", []), inc="d2_t")
                fr["v"] = [mt]
                mo = do("vector", lambda e: e.tensor_tensor(Zs[:, 0:n * F], X[:, 0:n * F], T[:, 0:n * F], ALU.add), mt, m_tr, inc="d2_o")
                fr[f"x{i % 2}"] = [mo]
                yield
                ks = transposes(lambda j, k: T[:, j * F + k * P:j * F + (k + 1) * P], n, [mt], "d2_tt")
                fr["T"] = [ks[-1][1], mo]
                mtT = copy_out("scalar", ks, TT, n, "d2_tc", [*m_x0, *fr.get(f"tT{i % 2}", [])])
                tick()
                yield
                q = take()
                for j in range(n):
                    for k in range(2):
                        m = do("tensor", lambda e, q=q, j=j, k=k: e.matmul(
                            psum[q][:, j * 8:j * 8 + 8], TT[:, k * 512 + j * P:k * 512 + (j + 1) * P], rwT[:, k, :],
                            start=k == 0, stop=k == 1), mtT, m_rw, *free[q], inc="d2_lg" if (j == n - 1 and k) else None)
                L = psum[q][:, 0:8 * n].rearrange("p (b e) -> p b e", e=8)

                def r(at, w=1):
                    return rt[:, at:at + n * w] if w == 1 else rt[:, at:at + n * w].rearrange("p (b e) -> p b e", e=w)

                def wide(a):
                    return a.rearrange("p (b o) -> p b o", o=1).broadcast_to([P, n, 8])
                p8, m8 = r(8, 8), r(48, 8)
                ix, ixf = rt[:, 88:88 + 8 * n].bitcast(U32), r(128, 8)
                m = do("vector", lambda e: e.tensor_reduce(r(0), L, AX.X, ALU.max), m, *m_x0, *fr.get("rt", []), inc="rt")
                m = do("vector", lambda e: e.tensor_tensor(p8, L, wide(r(0)), ALU.subtract), m, inc="rt")
                free[q] = [m]
                m = do("scalar", lambda e: e.activation(p8, p8, ACT.Exp), m, inc="rt_e")
                m = do("vector", lambda e: e.tensor_reduce(r(0), p8, AX.X, ALU.add), m, inc="rt")
                m = do("vector", lambda e: e.reciprocal(r(4), r(0)), m, inc="rt")
                m = do("vector", lambda e: e.tensor_tensor(p8, p8, wide(r(4)), ALU.mult), m, inc="rt")
                for j in range(n):
                    m1 = do("vector", lambda e, j=j: e.max(m8[:, j, :], p8[:, j, :]), m, inc="rt")
                for j in range(n):
                    m = do("vector", lambda e, j=j: e.max_index(ix[:, 8 * j:8 * j + 8], m8[:, j, :], p8[:, j, :]), m1, inc="rt")
                do("vector", lambda e: e.tensor_copy(rt[:, 128:128 + 8 * n], ix), m, inc="rt")
                m = do("vector", lambda e: e.tensor_tensor(r(0), m8[:, :, 0], m8[:, :, 1], ALU.add), m, inc="rt")
                m = do("vector", lambda e: e.tensor_scalar(r(0), r(0), 1e-12, None, ALU.max), m, inc="rt")
                m = do("vector", lambda e: e.reciprocal(r(4), r(0)), m, inc="rt")
                m = do("vector", lambda e: e.tensor_tensor(m8, m8, wide(r(4)), ALU.mult), m, inc="rt")
                g0, g1 = r(168, 8), r(208, 8)
                for j in range(n):
                    do("vector", lambda e, j=j: e.tensor_scalar(g0[:, j, :], iota_f[:, 0:8], ixf[:, j, 0:1], m8[:, j, 0:1],
                                                                ALU.is_equal, ALU.mult), m, inc="rt")
                    m1 = do("vector", lambda e, j=j: e.tensor_scalar(g1[:, j, :], iota_f[:, 0:8], ixf[:, j, 1:2], m8[:, j, 1:2],
                                                                     ALU.is_equal, ALU.mult), inc="rt")
                mcb = do("vector", lambda e: e.tensor_tensor(C[:, 0:8 * n].rearrange("p (b e) -> p b e", e=8), g0, g1, ALU.add),
                         m1, *fr.get(f"c{i % 2}", []), inc="rt")
                fr["rt"] = [mcb]
                tick()
                yield
                q = take()
                for j in range(n):
                    m = do("tensor", lambda e, q=q, j=j: e.transpose(psum[q][0:8, j * P:(j + 1) * P], C[:, 8 * j:8 * j + 8], ident[:, :]),
                           mcb, *free[q], inc="d2_ct" if j == n - 1 else None)
                m = do("scalar", lambda e, q=q: e.activation(cT[:, 0:n * P], psum[q][0:8, 0:n * P], ACT.Copy), m, *m_x0, *fr.get("cT", []), inc="d2_cc")
                free[q] = [m]
                yield
                for h in range(0, n, 2):
                    q = take()
                    for j in range(h, h + 2):
                        mb = do("tensor", lambda e, q=q, j=j, h=h: e.matmul(
                            psum[q][:, (j - h) * F:(j - h + 1) * F], cT[:, j * P:(j + 1) * P], b2s[:, :], start=True, stop=True),
                            m, m_b2, *free[q], inc="d2_b2" if j > h else None)
                    mo = do("vector", lambda e, q=q, h=h: e.tensor_tensor(Zs[:, h * F:(h + 2) * F], Zs[:, h * F:(h + 2) * F], psum[q][:, :], ALU.add),
                            mb, mo, inc="d2_o2")
                    free[q] = [mo]
                    tick()
                fr["cT"] = [mb]
                self.ready[i] = (mtT, mcb, mo)

            def experts(self, i, nxt):
                fr, Zs, tick = self.fr, self.Z(i), self.tick
                b0, n = SBS[i]
                mtT, mcb, mo0 = self.ready.pop(i)
                mo = [mo0]
                TT, C = self.tT[i % 2], self.comb[i % 2]
                up = {}

                def layer1(ex):
                    H = self.hT[ex % 2]
                    for m_ in range(2):
                        q = take()
                        for k in range(2):
                            m = do("tensor", lambda e, q=q, k=k, m_=m_: e.matmul(
                                psum[q][:, 0:n * P], self.w1s[:, ex, k, m_ * P:(m_ + 1) * P], TT[:, k * 512:k * 512 + n * P],
                                start=k == 0, stop=k == 1), mtT, self.m_ex, *free[q], inc="l1" if k else None)
                            tick()
                        fr[f"tT{i % 2}"] = [m]
                        mg = do("scalar", lambda e, q=q, m_=m_: e.activation(
                            H[:, m_ * 512:m_ * 512 + n * P], psum[q][:, 0:n * P], ACT.Gelu, bias=b1T[:, ex, m_:m_ + 1]),
                            m, m_b1, *fr.get(f"hT{ex % 2}", []), inc="gelu")
                        free[q] = [mg]
                    up[ex] = mg

                def layer2(ex):
                    H = self.hT[ex % 2]
                    new = None
                    for h in range(0, n, 2):
                        q = take()
                        for j in range(h, h + 2):
                            for k in range(2):
                                m = do("tensor", lambda e, q=q, j=j, h=h, k=k: e.matmul(
                                    psum[q][:, (j - h) * F:(j - h + 1) * F], H[:, k * 512 + j * P:k * 512 + (j + 1) * P],
                                    self.w2s[:, ex, k, :], start=k == 0, stop=k == 1), up[ex], *free[q],
                                    inc="l2" if (j > h and k) else None)
                            tick()
                        fr[f"hT{ex % 2}"] = [m]
                        for j in range(h, h + 2):
                            a = Zs[:, j * F:(j + 1) * F]
                            new = do("vector", lambda e, q=q, j=j, h=h, a=a: e.scalar_tensor_tensor(
                                a, psum[q][:, (j - h) * F:(j - h + 1) * F], C[:, 8 * j + ex:8 * j + ex + 1], a,
                                ALU.mult, ALU.add), m, mo[0], mcb, inc="moe")
                        free[q] = [new]
                    mo[0] = new

                layer1(0)
                for ex in range(NEXP):
                    if ex + 1 < NEXP:
                        layer1(ex + 1)
                    next(nxt, None)
                    layer2(ex)
                for _ in nxt:
                    pass
                fr[f"c{i % 2}"] = [mo[0]]
                nf = n - 1 if i == ns - 1 else n
                ms = dma("sync", out[b0 * P:(b0 + nf) * P, :].rearrange("(b p) f -> p b f", p=P),
                         Zs[:, 0:nf * F].rearrange("p (b f) -> p b f", f=F), mo[0], inc=f"st_o{i % 4}")
                if nf < n:
                    ms = dma("sync", out[(NB - 1) * P:N, :], Zs[0:LAST, nf * F:n * F], mo[0], inc=f"st_o{i % 4}")
                fr[f"Z{i % 4}"] = [ms]

            def stored(self):
                return [(f"st_o{k}", Q.count[f"st_o{k}"]) for k in range(4)]

        def general():
            m = do("vector", lambda e: e.tensor_scalar(s_tot, cum[:, NG - 1:NG], 127.0, None, ALU.add), m_cum, inc="base")
            m = do("vector", lambda e: e.tensor_copy(s_nI, s_tot), m, inc="base")
            m = do("vector", lambda e: e.tensor_single_scalar(s_nI, s_nI, 7, op=ALU.logical_shift_right), m, inc="base")
            m = do("vector", lambda e: e.tensor_copy(s_n, s_nI), m, inc="base")
            m = do("tensor", lambda e: e.matmul(psum[0][0:NB, 0:1], lowT[0:NB, 0:NB], s_n, start=True, stop=True), m, *free[0], inc="scp")
            m = do("vector", lambda e: e.tensor_copy(s_sc, psum[0][0:NB, 0:1]), m, inc="base")
            free[0] = [m]
            m = do("vector", lambda e: e.tensor_scalar(s_sc128, s_sc, 128.0, None, ALU.mult), m, inc="base")
            m_gb = do("vector", lambda e: e.tensor_scalar(gb, gb, s_sc128, None, ALU.add), m, inc="base")
            scat, rk = scatter([m_gb], NCOL, tabd, m_fill, False)
            half = NCOL // 2
            ci = bkf[0:NB, 0:half].bitcast(I32)
            ge = Bt[0][0:NB, 0:half]
            for k in range(2):
                mi = do("gpsimd", lambda e, k=k: e.iota(ci, pattern=[[1, half]], base=k * half, channel_multiplier=0),
                        *scat, *([("bmap", 1)] if k else []), inc="iotac")
                mm = do("vector", lambda e: e.tensor_scalar(ge, ci, s_sc, None, ALU.is_ge),
                        mi, rk, *([("bmap_p", 1)] if k else []), inc="bmap")
                for h in range(2):
                    pm = do("tensor", lambda e, h=h: e.matmul(psum[1 + h][0:1, 0:440], onesb[0:NB, 0:1], ge[:, h * 440:(h + 1) * 440],
                            start=True, stop=True), mm, *free[1 + h], *([("bmap", 2)] if k else []), inc="bmap_p" if h else None)
                for h in range(2):
                    at = k * half + h * 440
                    m_bk = do("vector", lambda e, h=h, at=at: e.tensor_scalar(
                        bkI[0:1, at:at + 440], psum[1 + h][0:1, 0:440], -1.0, float(F), ALU.add, ALU.mult), pm,
                        inc="bmap" if h else None)
            for k in range(8):
                free[k] = [*free[k], m_bk]

            cut = Cut(R0)
            tab = cut(NCOL * 4)
            tab3 = tab.rearrange("p (c k) -> p c k", k=4)
            GR, SR = 12, 6
            G = [cut(F) for i in range(GR)]
            S = [cut(P) for i in range(SR)]
            aT = [cut(1024) for i in range(2)]
            sq = [cut(512) for i in range(2)]
            m = dma("sync", tab, tab_rows, *scat, m_bk, inc="ld_tab")
            m_tab = do("vector", lambda e: e.tensor_copy(tab3[:, :, 3].bitcast(I32), tab3[:, :, 0]), m, inc="tabi")

            def aggregate(t, hd, *ready):
                mg, ms, mm, ma, regs = {}, {}, {}, {}, {}
                wait("gpsimd", m_tab, *ready)
                wait("vector", m_tab, *ready)

                def load(c):
                    n = min(RL, CH - c)

                    def go(e):
                        _, v = nc.values_load_multi_w_load_instructions(
                            bkI[0:1, c:c + n], engines=[e.engine], min_val=0, max_val=(NB - 1) * F,
                            skip_runtime_bounds_check_because="a count of blocks, 1 to NB, less one, times F")
                        for k in range(n):
                            regs[c + k] = v[k]
                    Q.q["vector"].append(go)

                def add(c):
                    if c % RL == 0:
                        load(c)

                    def go(e):
                        a = acc[:, bass.ds(regs[c], F)]
                        return e.tensor_tensor(a, psum[c % PR][:, 0:F], a, ALU.add)
                    ma[c] = do("vector", go, mm[c], *([ma[c - 1]] if c else []), inc=f"{t}_add")

                LAG = 4
                for c in range(CH + LAG):
                    if c < CH:
                        prev = [mm[c - GR]] if c >= GR else []
                        mg[c] = do("gpsimd", lambda e, c=c: e.indirect_dma_start(
                            G[c % GR], None, hd, bass.IndirectOffsetOnAxis(ap=tab3[:, c, 3:4].bitcast(I32), axis=0)),
                            *prev, inc=f"gat{c % GR}", by=16)
                        prev = [mm[c - SR]] if c >= SR else []
                        ms[c] = do("vector", lambda e, c=c: e.tensor_scalar(
                            S[c % SR], iota_f[:, :], tab3[:, c, 1:2], tab3[:, c, 2:3], ALU.is_equal, ALU.mult),
                            *prev, inc=f"{t}_sel")
                        prev = [ma[c - PR]] if c >= PR else free[c % PR]
                        mm[c] = do("tensor", lambda e, c=c: e.matmul(psum[c % PR][:, 0:F], S[c % SR], G[c % GR], start=True, stop=True),
                                   mg[c], ms[c], *prev, inc=f"{t}_mm")
                    if c >= LAG:
                        add(c - LAG)
                for k in range(8):
                    free[k] = [ma[CH - 1]]
                return mm[CH - 1], ma[CH - 1]

            pe1, agg1 = aggregate("a1", h1, m_h1, m_bk)
            a_free = {}
            for i in range(ns):
                my = dense1_y(i, [agg1], aT, a_free, "vector")
            m_h2, m_hc = dense1_rest(my, aT, sq, a_free)
            pe2, agg2 = aggregate("a2", h2, m_h2, m_hc)
            D = Dense2(Cut(R0), lambda i: acc_b(*SBS[i]))
            D.weights(pe2, agg2)
            for _ in D.first(0, [agg2], [pe2, agg2]):
                pass
            for i in range(ns):
                D.experts(i, D.first(i + 1, [agg2], [agg2]) if i + 1 < ns else iter(()))
            wait("sync", *D.stored(), m_fillm, m_offd, m_W1)

        def ordered():
            m = do("vector", lambda e: e.tensor_scalar(s_sc128, iota_p[0:NB, :], float(KC * P), None, ALU.mult), m_cum, inc="base")
            m_gb = do("vector", lambda e: e.tensor_scalar(gb, gb, s_sc128, None, ALU.add), m, inc="base")
            scat, rk = scatter([m_gb], NCF, msgd, m_fillm, True)
            tab = M[:, TOP - 3 * NCF:TOP]
            tab3 = tab.rearrange("p (c k) -> p c k", k=3)
            cut = Cut(R0, TOP - 3 * NCF)
            LR, SR = 3, 6
            L = [cut(KC * RW) for i in range(LR)]
            aT = [cut(1024) for i in range(2)]
            S = [cut(P) for i in range(SR)]
            sq = [L[0][:, 0:512], L[0][:, 512:1024]]
            for k in range(8):
                free[k] = [*free[k], rk]
            turn[0], turn[1], turn[2] = 0, 2, 8
            m_l, m_mm, m_cp, m_ad, mms = {}, {}, {}, {}, {}
            a_free = {}
            c = 0

            def load(b):
                m_l[b] = dma("sync", L[b % LR], msg3[:, b * KC:(b + 1) * KC, :].rearrange("p k r -> p (k r)"),
                             *scat, *([m_mm[b - LR], m_cp[b - LR]] if b >= LR else [rk]), inc=f"ldm{b % LR}")
            for b in range(LR):
                load(b)
            for b in range(NB):
                L3 = L[b % LR].rearrange("p (k r) -> p k r", r=RW)
                q = b % 2
                for k in range(KC):
                    prev = [mms[c - SR]] if c >= SR else [rk, *scat]
                    ms = do("vector", lambda e, c=c, k=k, L3=L3: e.tensor_scalar(
                        S[c % SR], iota_f[:, :], L3[:, k, F + 1:F + 2], L3[:, k, F + 2:F + 3], ALU.is_equal, ALU.mult),
                        m_l[b], *prev, inc="r_sel")
                    mms[c] = do("tensor", lambda e, c=c, k=k, L3=L3, q=q: e.matmul(
                        psum[q][:, 0:F], S[c % SR], L3[:, k, 0:F], start=k == 0, stop=k == KC - 1),
                        ms, *free[q], inc="r_mm")
                    c += 1
                m_mm[b] = mms[c - 1]
                m_cp[b] = do("gpsimd", lambda e, b=b, L3=L3: e.tensor_copy(tab3[:, b * KC:(b + 1) * KC, :], L3[:, :, F:F + 3]),
                             m_l[b], inc="r_tab")
                m_ad[b] = do("vector", lambda e, b=b, q=q: e.tensor_tensor(acc_b(b), acc_b(b), psum[q][:, 0:F], ALU.add),
                             m_mm[b], inc="r_add")
                free[q] = [m_ad[b]]
                if b + LR < NB:
                    load(b + LR)
                if b and (b % SB == 0):
                    my = dense1_y(b // SB - 1, [m_ad[b - 1]], aT, a_free, "scalar")
            my = dense1_y(ns - 1, [m_ad[NB - 1]], aT, a_free, "scalar")
            turn[0], turn[1], turn[2] = 0, 0, 8
            wait("scalar", m_cp[NB - 1])
            m_h2, m_hc = dense1_rest(my, aT, sq, a_free)

            turn[0], turn[1], turn[2] = 0, 2, 8
            cut = Cut(0, TOP - 3 * NCF)
            idx = cut(NCF).bitcast(I32)
            GR, S2R = 20, 8
            G = [cut(F) for i in range(GR)]
            S2 = [cut(P) for i in range(S2R)]
            Zb = [cut(1024) for i in range(4)]
            all_pe = ("d1_bt", Q.count["d1_bt"])
            m_idx = do("vector", lambda e: e.tensor_copy(idx, tab3[:, :, 0]), m_cp[NB - 1], m_h2, inc="idx")
            wait("sync", m_h2, all_pe)
            wait("gpsimd", m_h2, all_pe, m_idx)
            wait("vector", m_h2, all_pe)
            mg, ms, mm, m_sf, m_z = {}, {}, {}, {}, {}
            LEAD = 4

            def gather(c):
                prev = [mm[c - GR]] if c >= GR else []
                mg[c] = do("gpsimd", lambda e: e.indirect_dma_start(
                    G[c % GR], None, h2, bass.IndirectOffsetOnAxis(ap=idx[:, c:c + 1], axis=0)),
                    *prev, inc=f"gat{c % GR}", by=16)

            def select(c):
                prev = [mm[c - S2R]] if c >= S2R else []
                ms[c] = do("vector", lambda e: e.tensor_scalar(
                    S2[c % S2R], iota_f[:, :], tab3[:, c, 1:2], tab3[:, c, 2:3], ALU.is_equal, ALU.mult), *prev, inc="g_sel")

            for c in range(GR):
                gather(c)
            for c in range(LEAD):
                select(c)

            def chunks(i):
                b0, n = SBS[i]
                Zs = Zb[i % 4]
                nf = n if i < ns - 1 else n - 1
                old = D.fr.get(f"Z{i % 4}", [])
                m_s = dma("sync", Zs[:, 0:nf * F].rearrange("p (b f) -> p b f", f=F),
                          h2[b0 * P:(b0 + nf) * P, :].rearrange("(b p) f -> p b f", p=P), *old, inc=f"ld_z{i % 4}")
                if nf < n:
                    mz = do("vector", lambda e: e.memset(Zs[:, nf * F:n * F], 0.0), *old, inc="zz")
                    m_s = dma("sync", Zs[0:LAST, nf * F:n * F], h2[(NB - 1) * P:N, :], mz, inc=f"ld_z{i % 4}")
                for b in range(b0, b0 + n):
                    q = b % 2
                    for k in range(KC):
                        c = b * KC + k
                        if c + LEAD < NCF:
                            select(c + LEAD)
                        mm[c] = do("tensor", lambda e, c=c, k=k, q=q: e.matmul(
                            psum[q][:, 0:F], S2[c % S2R], G[c % GR], start=k == 0, stop=k == KC - 1),
                            mg[c], ms[c], *free[q], inc="g_mm")
                        if c + GR < NCF:
                            gather(c + GR)
                        if k < KC - 1:
                            yield
                    j = b - b0
                    m_z[i] = do("vector", lambda e, j=j, q=q: e.tensor_tensor(
                        Zs[:, j * F:(j + 1) * F], Zs[:, j * F:(j + 1) * F], psum[q][:, 0:F], ALU.add), mm[c], m_s, inc="g_add")
                    free[q] = [m_z[i]]
                    yield

            flow = [iter(())]
            D = Dense2(cut, lambda i: Zb[i % 4][:, 0:SBS[i][1] * F], lambda: next(flow[0], None))
            D.weights()
            for t in range(ns + 2):
                flow[0] = chunks(t) if t < ns else iter(())
                nxt = D.first(t - 1, [m_z[t - 1]], []) if 1 <= t <= ns else iter(())
                if t >= 2:
                    D.experts(t - 2, nxt)
                for _ in nxt:
                    pass
                for _ in flow[0]:
                    pass
            wait("sync", *D.stored(), m_fill)

        fast = Q.path(ordered)
        for k in range(8):
            free[k] = [m_cum, m_pre, m_flag]
        turn[0], turn[1], turn[2] = 0, 0, 8
        slow = Q.path(general)
        Q.run(ctx.enter_context(nc.Block()), nc, flagI, m_flag, fast, slow)


_INS = ["x", "src", "dst", "edge_weight", "L0_gnn_W1", "L0_gnn_W2", "L0_gnn_gamma", "L0_gnn_beta",
        "L0_ffn_router_w", "L0_ffn_w1", "L0_ffn_b1", "L0_ffn_w2", "L0_ffn_b2"]


def kernel(**inputs):
    import numpy as np
    import concourse.bacc as bacc
    from concourse.bass_utils import run_bass_kernel_spmd

    nc = bacc.Bacc("TRN2", target_bir_lowering=False, num_devices=1)
    arrays, args = {}, []
    for name in _INS:
        a = np.ascontiguousarray(inputs[name])
        arrays[f"in_{name}"] = a
        args.append(nc.dram_tensor(f"in_{name}", a.shape, mybir.dt.from_np(a.dtype), kind="ExternalInput").ap())
    out = nc.dram_tensor("out_0", (N, F), F32, kind="ExternalOutput").ap()
    build(nc, *args, out)
    r = run_bass_kernel_spmd(nc, [arrays], core_ids=[0])
    return r.results[0]["out_0"]
```

```python
import concourse.bass as bass
from concourse import mybir
from contextlib import ExitStack

F32 = mybir.dt.float32
FR = mybir.dt.float32r
BF16 = mybir.dt.bfloat16
I32 = mybir.dt.int32
U32 = mybir.dt.uint32
ALU = mybir.AluOpType
ACT = mybir.ActivationFunctionType
AX = mybir.AxisListType

N = 12500
F = 256
E = 212500
P = 128
R = 125
NB = N // R
PE_P = 125
EC = 1700
GC = 5
NG = EC // GC
GE = GC * PE_P
TG, PG = 4, 85
SG = 20
NSG = EC // SG
KC = 18
NCF = NB * KC
KLO = 15
GF = 199
HI, LO = 13, 8
CG = 85
RW = F + 4
CH = (E + NB * 127) // 128
NCOL = 1760
XB = 10
NX = NB // XB
SB = 4
SBS = [(b, SB) for b in range(0, NB - SB, SB)] + [(NB - 4, 2), (NB - 2, 2)]
NEXP = 8
EPS = 1e-05
PR = 8
MR = 4
RL = 8


class Queues:

    def __init__(self, nc, ctx):
        self.nc, self.ctx = nc, ctx
        self.sems, self.count, self.passed = {}, {}, {}
        self.q = self.fresh()

    def fresh(self):
        return {"sync": [], "scalar": [], "vector": [], "tensor": [], "gpsimd": []}

    def sem(self, name):
        if name not in self.sems:
            self.sems[name] = self.ctx.enter_context(self.nc.semaphore(name))
        return self.sems[name]

    def wait(self, eng, *marks):
        for name, value in marks:
            if self.passed.get((eng, name), 0) < value:
                self.passed[(eng, name)] = value
                s = self.sem(name)
                self.q[eng].append(lambda e, s=s, value=value: e.wait_ge(s, value))

    def do(self, eng, fn, *marks, inc=None, by=1):
        self.wait(eng, *marks)
        if inc is None:
            self.q[eng].append(fn)
            return None
        s = self.sem(inc)
        self.count[inc] = self.count.get(inc, 0) + by
        self.q[eng].append(lambda e, s=s: fn(e).then_inc(s, by))
        return inc, self.count[inc]

    def dma(self, eng, out, in_, *marks, inc):
        return self.do(eng, lambda e: e.dma_start(out, in_), *marks, inc=inc, by=16)

    def rows(self, eng, out, in_, *marks, inc):
        for a, b in ((0, 112), (112, R)):
            m = self.dma(eng, out[a:b], in_[a:b], *marks, inc=inc)
        return m

    def path(self, make):
        kept = self.q, dict(self.count), dict(self.passed)
        self.q = self.fresh()
        make()
        made = self.q
        self.q, self.count, self.passed = kept
        return made

    def run(self, block, nc, flag, m_flag, fast, slow):
        for name in self.q:
            self.wait(name, m_flag)
            {"sync": block.sync, "scalar": block.scalar, "vector": block.vector,
             "tensor": block.tensor, "gpsimd": block.gpsimd}[name](
                lambda eng, name=name: self.body(eng, nc, name, flag, fast, slow))

    def body(self, eng, nc, name, flag, fast, slow):
        for fn in self.q[name]:
            fn(eng)
        v = nc.values_load(flag, engines=[eng.engine], min_val=0, max_val=1,
                           skip_runtime_bounds_check_because="a minimum with 1 of a count")
        with eng.If(v == 0):
            for fn in fast[name]:
                fn(eng)
        with eng.Else():
            for fn in slow[name]:
                fn(eng)


def build(nc, x, src, dst, ew, W1, W2, gamma, beta, rw, w1, b1, w2, b2, out, force=None):
    h1 = nc.dram_tensor("h1", (N, F), F32, kind="Internal").ap()
    h2 = nc.dram_tensor("h2", (N, F), F32, kind="Internal").ap()
    tabd = nc.dram_tensor("tabd", (P * NCOL, 4), F32, kind="Internal").ap()
    tab_rows = tabd.rearrange("(p c) k -> p (c k)", p=P)
    msgd = nc.dram_tensor("msgd", (P * NCF, RW), F32, kind="Internal").ap()
    msg3 = msgd.rearrange("(p c) k -> p c k", p=P)
    offd = nc.dram_tensor("offd", (1, E), BF16, kind="Internal").ap()

    with ExitStack() as ctx:
        Q = Queues(nc, ctx)
        do, dma, wait, rows_ = Q.do, Q.dma, Q.wait, Q.rows

        def sb(name, shape, dt=F32):
            return ctx.enter_context(nc.sbuf_tensor(name, shape, dt))

        ident = sb("ident", [P, P])
        iota_f = sb("iota_f", [P, P])
        iota_p = sb("iota_p", [P, 1])
        W1s = sb("W1s", [P, 2, F])
        W2s = sb("W2s", [P, 2, F])
        gbT = sb("gbT", [P, 4])
        rwT = sb("rwT", [P, 2, NEXP])
        b1T = sb("b1T", [P, NEXP, 2])
        b2s = sb("b2s", [NEXP, F])
        pre = sb("pre", [36, P])
        small = sb("small", [P, 960])
        tabT = sb("tabT", [P, 3 * NCF])
        psum = [ctx.enter_context(nc.psum_tensor(f"ps{i}", [P, 512], F32)) for i in range(8)]

        class Cut:

            def __init__(self, t):
                self.t, self.at, self.end = t, 0, t.shape[1]

            def __call__(self, n, p=P):
                a = self.at
                self.at += n
                assert self.at <= self.end, (self.at, self.end)
                return self.t[0:p, a:a + n]

        phase = ExitStack()
        inner = ExitStack()
        acc = phase.enter_context(nc.sbuf_tensor("acc", [P, NB * F], F32))
        XW = 19520
        X0 = inner.enter_context(nc.sbuf_tensor("X0", [P, XW], F32))
        cut = Cut(X0)
        bkI = X0[0:1, XW - NCOL:XW].bitcast(I32)
        bkf = cut(EC, PE_P)
        rec = cut(EC * 4, PE_P)
        rec3 = rec.rearrange("p (c k) -> p c k", k=4)
        raw = Cut(X0)
        raw.at = cut_d = cut.at
        NBB = 3
        NDG = 4
        dg = [cut(NB, NB) for i in range(NDG)]
        junk = [cut(NB, PE_P) for i in range(2 * GC)]
        WR = 3
        Win = [cut(F) for i in range(WR)]
        offb = [cut((GE + 1) // 2).bitcast(BF16)[:, 0:GE] for i in range(WR)]
        OH = [cut(GE) for i in range(2)]
        msg = [cut(GC * RW, PE_P) for i in range(MR)]
        rS, rB, rD, rW = raw(TG * GE, PG), raw(TG * GE, PG), raw(TG * GE, PG), raw(TG * GE, PG)
        offm = rec[0:PG, 0:TG * GE]
        offs = rec[0:PG, TG * GE:TG * GE + TG * GE // 2].bitcast(BF16)
        cut = Cut(tabT)
        ones = cut(P)
        lowT = cut(P)
        onesb = cut(P // 2).bitcast(BF16)
        lowb = cut(P // 2).bitcast(BF16)
        cum = cut(NG, NB)
        gb = cut(NG, NB)
        zrow = cut(1040)
        Bt = [cut(SG * NB // 2, PE_P).bitcast(BF16) for i in range(NBB)]
        Bl = [b[:, CG * HI + 1:CG * HI + 1 + CG * LO] for b in Bt]
        s_tot = small[0:NB, 0:1]
        s_nI = small[0:NB, 1:2].bitcast(I32)
        s_n = small[0:NB, 2:3]
        s_sc = small[0:NB, 3:4]
        s_sc128 = small[0:NB, 5:6]
        r0f = small[0:PG, 8:8 + TG]
        r0I = small[0:TG, 16:16 + PG].bitcast(I32)
        viol = small[:, 104:109]
        flagI = small[0:1, 110:111].bitcast(I32)
        posf = small[0:PE_P, 112:112 + MR * GC]
        posA = small[0:PE_P, 136:136 + 3 * GC].bitcast(I32)
        posI = small[0:PE_P, 152:152 + MR * GC].bitcast(I32)
        stats = small[0:R, 176:176 + XB * 6]
        mv = small[0:R, 264:264 + XB * 2]
        nrm = small[0:R, 296:296 + XB * 2]

        def acc_b(b, n=1):
            return acc[0:R, b * F:(b + n) * F]

        free = [[] for _ in range(8)]
        turn = [0, 0, 8]

        def take():
            i = turn[1] + turn[0] % (turn[2] - turn[1])
            turn[0] += 1
            return i

        m = do("gpsimd", lambda e: e.iota(iota_f[:, :].bitcast(I32), pattern=[[1, P]], base=0, channel_multiplier=0), inc="cst")
        m_iota = do("vector", lambda e: e.tensor_copy(iota_f[:, :], iota_f[:, :].bitcast(I32)), m, inc="cstb")
        m = do("gpsimd", lambda e: e.iota(iota_p[:, :].bitcast(I32), pattern=[[0, 1]], base=0, channel_multiplier=1), inc="cst")
        m_iotap = do("vector", lambda e: e.tensor_copy(iota_p[:, :], iota_p[:, :].bitcast(I32)), m, inc="cstb")
        do("gpsimd", lambda e: e.memset(ident[:, :], 0.0), inc="cst")
        m2 = do("gpsimd", lambda e: e.memset(ones, 1.0), inc="cst")
        m_ident = do("gpsimd", lambda e: e.affine_select(out=ident[:, :], in_=ident[:, :], compare_op=ALU.not_equal, fill=1.0,
                     base=0, pattern=[[-1, P]], channel_multiplier=1), m2, inc="cst")
        m_low = do("gpsimd", lambda e: e.affine_select(out=lowT, in_=ones, compare_op=ALU.is_gt, fill=0.0,
                   base=0, pattern=[[1, P]], channel_multiplier=-1), m_ident, inc="cst")
        m_zrow = do("gpsimd", lambda e: e.memset(zrow, 0.0), inc="cst")
        do("vector", lambda e: e.tensor_copy(onesb, ones), m_low, inc="cstb")
        m_cstb = do("vector", lambda e: e.tensor_copy(lowb, lowT), inc="cstb")
        m_vz = do("vector", lambda e: e.memset(viol, 0.0), inc="cstb")

        def run4(a):
            return a.rearrange("(t p k) -> p t k", t=TG, p=PG)

        m_src = dma("sync", rS.bitcast(I32).rearrange("p (t k) -> p t k", t=TG), run4(src), inc="ld_src")
        m_dst = dma("sync", rD.bitcast(I32).rearrange("p (t k) -> p t k", t=TG), run4(dst), inc="ld_dst")
        m_ew = dma("sync", rW.rearrange("p (t k) -> p t k", t=TG), run4(ew), inc="ld_w")

        m_x = []
        for i in range(NX):
            b0 = i * XB
            m = rows_("scalar", acc_b(b0, XB).rearrange("p (b f) -> p b f", f=F),
                    x[b0 * R:(b0 + XB) * R, :].rearrange("(b p) f -> p b f", p=R), inc=f"ld_x{i}")
            m_x.append(m)

        m3 = msg3.rearrange("p (b k) r -> p b (k r)", k=KC)
        zw = zrow[:, :].rearrange("p (o r) -> p o r", o=1)
        fills = [(m3[:, b:b + 2, KLO * RW:KC * RW], zw[:, :, 0:(KC - KLO) * RW].broadcast_to([P, 2, (KC - KLO) * RW]))
                 for b in range(0, NB, 2)]
        m_fillm = ("fillm", 16 * len(fills))

        rSI, rBI, rDI = rS.bitcast(I32), rB.bitcast(I32), rD.bitcast(I32)
        m = do("vector", lambda e: e.tensor_copy(rS, rSI), m_src, inc="edg")
        m = do("vector", lambda e: e.tensor_scalar(rB, rS, 1.0 / R, 0.5 / R - 0.5, ALU.mult, ALU.add), m, inc="edg")
        m = do("vector", lambda e: e.tensor_copy(rBI, rB), m, inc="edg")
        m = do("vector", lambda e: e.tensor_copy(rB, rBI), m, inc="edg")
        m = do("vector", lambda e: e.scalar_tensor_tensor(rS, rB, -float(R), rS, ALU.mult, ALU.add), m, inc="edg")
        m = do("vector", lambda e: e.tensor_copy(rD, rDI), m_dst, inc="edg")
        rD3 = rD.rearrange("p (t k) -> p t k", t=TG)
        m_r0 = do("vector", lambda e: e.tensor_scalar(r0f, rD3[:, :, 0], float(N - P), None, ALU.min), m, inc="edg")
        o3, om3 = offs.rearrange("p (t k) -> p t k", t=TG), offm.rearrange("p (t k) -> p t k", t=TG)
        for t in range(TG):
            m = do("vector", lambda e, t=t: e.tensor_scalar(om3[:, t, :], rD3[:, t, :], r0f[:, t:t + 1], None, ALU.subtract), m_r0, inc="edg")
        m_off = do("vector", lambda e: e.tensor_copy(offs, offm), m, inc="edg")
        do("vector", lambda e: e.tensor_reduce(viol[0:PG, 0:1], offm, AX.X, ALU.max), m_vz, inc="viol")
        m = do("vector", lambda e: e.tensor_reduce(viol[0:PG, 1:2], offm, AX.X, ALU.min), inc="viol")
        do("vector", lambda e: e.tensor_scalar(viol[0:PG, 0:1], viol[0:PG, 0:1], float(P - 1), None, ALU.is_gt), m, inc="viol")
        m_v1 = do("vector", lambda e: e.tensor_scalar(viol[0:PG, 1:2], viol[0:PG, 1:2], 0.0, None, ALU.is_lt), inc="viol")
        m_offd = dma("sync", offd.rearrange("o (t p k) -> p (o t) k", t=TG, p=PG), o3, m_off, inc="st_off")
        m = do("tensor", lambda e: e.transpose(psum[7][0:TG, 0:PG], r0f, ident[0:PG, 0:PG]), m_r0, m_ident, inc="r0")
        m_r0I = do("vector", lambda e: e.tensor_copy(r0I, psum[7][0:TG, 0:PG]), m, inc="r0c")
        free[7] = [m_r0I]

        for w, (raw_, mr, to) in enumerate([(rB, m_r0, bkf.rearrange("p (g j) -> p g j", j=GC)),
                                            (rD, m_r0, rec3[:, :, 0].rearrange("p (g j) -> p g j", j=GC)),
                                            (rS, m_r0, rec3[:, :, 1].rearrange("p (g j) -> p g j", j=GC)),
                                            (rW, m_ew, rec3[:, :, 2].rearrange("p (g j) -> p g j", j=GC))]):
            for t in range(TG):
                i = take()
                for j in range(GC):
                    m = do("tensor", lambda e, i=i, j=j, raw_=raw_, t=t: e.transpose(
                        psum[i][0:PE_P, j * PG:(j + 1) * PG], raw_[:, t * GE + j * PE_P:t * GE + (j + 1) * PE_P], ident[0:PG, 0:PG]),
                        mr, m_ident, *free[i], inc="etr" if j == GC - 1 else None)
                m_ec = do("vector", lambda e, i=i, t=t, to=to: e.tensor_copy(
                    to[:, t * PG:(t + 1) * PG, :], psum[i][0:PE_P, 0:GC * PG].rearrange("p (j g) -> p g j", j=GC)),
                    m, m_v1, *([m_offd] if w else []), inc="etc")
                free[i] = [m_ec]
            if w == 0:
                m_bkf = m_ec
        m_rec = do("vector", lambda e: e.memset(rec3[:, :, 3], 0.0), m_v1, m_offd, inc="etc")

        def norm_group(i):
            b0 = i * XB
            for j in range(XB):
                m = do("vector", lambda e, j=j: e.bn_stats(stats[:, 6 * j:6 * j + 6], acc_b(b0 + j)),
                       m_x[i], *([("ln_ab", i)] if i else []), inc="ln_st")
            for j in range(XB):
                m2 = do("vector", lambda e, j=j: e.bn_aggr(mv[:, 2 * j:2 * j + 2], stats[:, 6 * j:6 * j + 6]), m, inc="ln_st")
            mv3 = mv.rearrange("p (b k) -> p b k", k=2)
            m = do("vector", lambda e: e.tensor_scalar(nrm[:, 0:XB], mv3[:, :, 1], EPS, None, ALU.add),
                   m2, *([("ln_h", XB * i)] if i else []), inc="ln_st")
            m = do("scalar", lambda e: e.activation(nrm[:, 0:XB], nrm[:, 0:XB], ACT.Sqrt), m, inc="ln_sq")
            m = do("vector", lambda e: e.reciprocal(nrm[:, 0:XB], nrm[:, 0:XB]), m, inc="ln_st")
            m = do("vector", lambda e: e.scalar_tensor_tensor(nrm[:, XB:2 * XB], mv3[:, :, 0], -1.0, nrm[:, 0:XB], ALU.mult, ALU.mult),
                   m, inc="ln_ab")
            for j in range(XB):
                mh = do("scalar", lambda e, j=j: e.activation(acc_b(b0 + j), acc_b(b0 + j), ACT.Identity,
                        bias=nrm[:, XB + j:XB + j + 1], scale=nrm[:, j:j + 1]), m, inc="ln_h")
            rows_("sync", h1[b0 * R:(b0 + XB) * R, :].rearrange("(b p) f -> p b f", p=R),
                acc_b(b0, XB).rearrange("p (b f) -> p b f", f=F), mh, inc="st_h1")

        def onehot(i, *marks):
            c0 = (i % NSG) * SG
            Bv = Bt[i % NBB].rearrange("p (c b) -> p c b", b=NB)
            return do("vector", lambda e: e.tensor_tensor(
                Bv, bkf[:, c0:c0 + SG].rearrange("p (c o) -> p c o", o=1).broadcast_to([PE_P, SG, NB]),
                iota_f[0:PE_P, 0:NB].rearrange("p (o b) -> p o b", o=1).broadcast_to([PE_P, SG, NB]), ALU.is_equal),
                *marks, inc="oneh")

        dig = [X0[0:PE_P, cut_d + k * EC:cut_d + (k + 1) * EC] for k in range(2)]
        hiI, loI = (d.bitcast(I32) for d in dig)
        m = do("vector", lambda e: e.tensor_copy(loI, bkf), m_bkf, m_ec, inc="dig")
        m = do("vector", lambda e: e.tensor_single_scalar(hiI, loI, 3, op=ALU.logical_shift_right), m, inc="dig")
        m = do("vector", lambda e: e.tensor_single_scalar(loI, loI, LO - 1, op=ALU.bitwise_and), m, inc="dig")
        m = do("vector", lambda e: e.tensor_copy(dig[0], hiI), m, inc="dig")
        m_dig = do("vector", lambda e: e.tensor_copy(dig[1], loI), m, inc="dig")
        sel = X0[0:HI, cut_d + 2 * EC:cut_d + 2 * EC + LO * NB].rearrange("p (l b) -> p l b", l=LO)
        selv = small[0:HI, 112:112 + LO]
        for l in range(LO):
            m = do("vector", lambda e, l=l: e.tensor_scalar(selv[:, l:l + 1], iota_p[0:HI, :], float(LO), float(l), ALU.mult, ALU.add),
                   m_iotap, inc="dig")
        for l in range(LO):
            m_selr = do("vector", lambda e, l=l: e.tensor_scalar(sel[:, l, :], iota_f[0:HI, 0:NB], selv[:, l:l + 1], None, ALU.is_equal),
                        m, m_iota, m_ec, inc="dig")
        c2 = X0[0:HI, cut_d + 2 * EC + LO * NB:cut_d + 2 * EC + LO * NB + LO * NG].rearrange("p (l g) -> p l g", l=LO)
        GB = 60
        m_cnt, m_c2 = {}, []
        nxn = 0
        for i in range(EC // CG):
            Hv = Bt[i % NBB][:, 0:CG * HI].rearrange("p (c b) -> p c b", b=HI)
            Lv = Bl[i % NBB][:, 0:CG * LO].rearrange("p (c b) -> p c b", b=LO)
            old = [m_cnt[i - NBB]] if i >= NBB else []
            for V, w, d in ((Hv, HI, dig[0]), (Lv, LO, dig[1])):
                mb = do("vector", lambda e, V=V, w=w, d=d, i=i: e.tensor_tensor(
                    V, d[:, i * CG:(i + 1) * CG].rearrange("p (c o) -> p c o", o=1).broadcast_to([PE_P, CG, w]),
                    iota_f[0:PE_P, 0:w].rearrange("p (o b) -> p o b", o=1).broadcast_to([PE_P, CG, w]), ALU.is_equal),
                    m_dig, m_iota, *old, inc="oneh")
            for c in range(CG):
                g, j = (i * CG + c) // GC, (i * CG + c) % GC
                q, at = 1 + g // GB, (g % GB) * LO
                fin = c == CG - 1 or (j == GC - 1 and (g % GB == GB - 1 or g == NG - 1))
                m = do("tensor", lambda e, q=q, at=at, Hv=Hv, Lv=Lv, c=c, j=j: e.matmul(
                    psum[q][0:HI, at:at + LO], Hv[:, c, :], Lv[:, c, :], start=j == 0, stop=j == GC - 1), mb, *free[q], inc="cnt" if fin else None)
                if j == GC - 1 and (g % GB == GB - 1 or g == NG - 1):
                    g0 = g // GB * GB
                    m_c2.append(do("vector", lambda e, q=q, g0=g0, g=g: e.tensor_copy(
                        c2[:, :, g0:g + 1], psum[q][0:HI, 0:(g + 1 - g0) * LO].rearrange("p (g l) -> p l g", l=LO)), m, m_ec, inc="c2"))
                    free[q] = [m_c2[-1]]
            m_cnt[i] = m
            if i >= 8 and nxn < NX:
                norm_group(nxn)
                nxn += 1
        i0 = 0
        cnt = psum[i0][0:NB, 0:NG]
        for l in range(LO):
            m_cntz = do("tensor", lambda e, l=l: e.matmul(cnt, sel[:, l, :], c2[:, l, :], start=l == 0, stop=l == LO - 1),
                        m_c2[-1], m_selr, *free[i0], inc="cnt")
        m = m_cntz
        m = do("vector", lambda e: e.tensor_tensor_scan(cum, ones[0:NB, 0:1].broadcast_to([NB, NG]), cnt, 0.0, ALU.mult, ALU.add), m, inc="base")
        m_cum = do("vector", lambda e: e.tensor_tensor(gb, cum, cnt, ALU.subtract), m, inc="base")
        free[i0] = [m_cum]
        tot = cum[:, NG - 1:NG]
        do("vector", lambda e: e.tensor_scalar(viol[0:NB, 2:3], tot, float(KC * P), None, ALU.is_gt), m_cum, inc="viol")
        do("vector", lambda e: e.tensor_scalar(viol[0:NB, 3:4], tot, float(KLO * P), None, ALU.is_lt), inc="viol")
        m = do("vector", lambda e: e.tensor_scalar(viol[0:NB, 4:5], cum[:, GF:GF + 1], float(KLO * P), None, ALU.is_gt), inc="viol")
        i1 = take()
        m = do("tensor", lambda e: e.matmul(psum[i1][0:1, 0:5], ones[:, 0:1], viol, start=True, stop=True), m, *free[i1], inc="vsum")
        m = do("vector", lambda e: e.tensor_reduce(small[0:1, 109:110], psum[i1][0:1, 0:5], AX.X, ALU.add), m, inc="viol")
        free[i1] = [m]
        if force is not None:
            m = do("vector", lambda e: e.tensor_scalar(small[0:1, 109:110], small[0:1, 109:110], float(force), None, ALU.add), m, inc="viol")
        m_flag = do("vector", lambda e: e.tensor_scalar(flagI, small[0:1, 109:110], 1.0, None, ALU.min), m, inc="viol")

        m_W1 = dma("sync", W1s[:, :, :], W1.rearrange("(k p) f -> p k f", p=P), inc="ld_W1")
        m_W2 = dma("sync", W2s[:, :, :], W2.rearrange("(k p) f -> p k f", p=P), inc="ld_W2")
        rows = pre[:, :]
        dma("sync", rows[0:2, :], gamma.rearrange("(m p) -> m p", p=P), inc="ld_pre")
        dma("sync", rows[2:4, :], beta.rearrange("(m p) -> m p", p=P), inc="ld_pre")
        dma("sync", rows[4:20, :], b1.rearrange("e (m p) -> (e m) p", p=P), inc="ld_pre")
        m = dma("sync", rows[20:36, :], rw.rearrange("e (k p) -> (e k) p", p=P), inc="ld_pre")
        m_b2 = dma("sync", b2s[:, :], b2, inc="ld_b2")
        i2 = take()
        m = do("tensor", lambda e: e.transpose(psum[i2][:, 0:36], rows, ident[0:36, 0:36]), m, m_ident, *free[i2], inc="pre_t")
        do("vector", lambda e: e.tensor_copy(gbT[:, :], psum[i2][:, 0:4]), m, inc="pre_c")
        do("vector", lambda e: e.tensor_copy(b1T[:, :, :].rearrange("p e m -> p (e m)"), psum[i2][:, 4:20]), inc="pre_c")
        m_pre = do("vector", lambda e: e.tensor_copy(
            rwT[:, :, :], psum[i2][:, 20:36].rearrange("p (e k) -> p k e", k=2)), inc="pre_c")
        free[i2] = [m_pre]
        m_gbT = m_b1 = m_rw = m_pre
        m_h1 = ("st_h1", Q.count["st_h1"])

        def scatter(base_marks, ncol, target, m_filled, g_fill, expand):
            m_rk, m_sel, m_oh, m_ohx, m_scat, m_ev, m_w, m_of = {}, {}, {}, {}, {}, {}, {}, {}
            m_dg, m_B, m_sl = {}, {}, {}
            GS = SG // GC
            if expand:
                for k in range(MR):
                    mz = do("gpsimd", lambda e, k=k: e.memset(msg[k], 0.0), m_offd, m_ec, m_cntz, inc="msgz")

            def load(g):
                old = [m_ohx[g - WR]] if g >= WR else []

                def go(e):
                    t, p_ = divmod(g, PG)
                    _, v = nc.values_load_multi_w_load_instructions(
                        r0I[t:t + 1, p_:p_ + 1], engines=[e.engine], min_val=0, max_val=N - P,
                        skip_runtime_bounds_check_because="a node's number, at most N - P by a minimum")
                    return e.dma_start(Win[g % WR], h1[bass.ds(v[0], P), :])
                m_w[g] = do("sync", go, m_h1, m_r0I, m_offd, m_cntz, m_ec, *old, inc=f"win{g % WR}", by=16)
                m_of[g] = dma("sync", offb[g % WR], offd[:, g * GE:(g + 1) * GE].broadcast_to([P, GE]), *old, inc=f"ofb{g % WR}")

            def rank(g):
                i, c0 = g // GS, (g * GC) % SG
                k = NSG + i
                if g % GS == 0:
                    ob = [m_cntz] if i < NBB else [m_rk[(i - NBB + 1) * GS - 1]]
                    m_B[i] = onehot(k, *base_marks, *ob)
                md = do("vector", lambda e: e.tensor_scalar(dg[g % NDG], ident[0:NB, 0:NB], gb[:, g:g + 1], None, ALU.mult),
                        *base_marks, m_ident, *([m_rk[g - NDG]] if g >= NDG else [m_ec]), inc="diag")
                bank = psum[g % 3][0:PE_P, 0:GC * NB].rearrange("p (c b) -> p c b", b=NB)
                Bv = Bt[k % NBB].rearrange("p (c b) -> p c b", b=NB)
                do("tensor", lambda e: e.matmul(
                    bank, ones[0:NB, 0:PE_P], dg[g % NDG].rearrange("p (o b) -> p o b", o=1).broadcast_to([NB, GC, NB]),
                    start=True, stop=False), md, m_B[i], *([m_sel[g - 3]] if g >= 3 else free[g % 3]))
                for j in range(GC - 1):
                    do("tensor", lambda e, j=j: e.matmul(
                        bank[:, j + 1:GC, :], onesb[0:PE_P, 0:PE_P],
                        Bv[:, c0 + j:c0 + j + 1, :].broadcast_to([PE_P, GC - 1 - j, NB]), start=False, stop=False))
                m_rk[g] = do("tensor", lambda e: e.matmul(
                    bank, lowb[0:PE_P, 0:PE_P], Bv[:, c0:c0 + GC, :], start=False, stop=True), inc="rank")

            def slots(g):
                bank = psum[g % 3]
                r = g % MR
                for j in range(GC):
                    c = g * GC + j
                    m = do("vector", lambda e, c=c, j=j: e.scalar_tensor_tensor(
                        junk[c % (2 * GC)], iota_f[0:PE_P, 0:NB], bkf[:, c:c + 1], bank[0:PE_P, j * NB:(j + 1) * NB],
                        ALU.is_equal, ALU.mult, accum_out=posf[:, r * GC + j:r * GC + j + 1]), m_rk[g], m_rec,
                        *([m_sel[g - 2]] if g >= 2 else []), *([m_sl[g - 1]] if g else []), inc="sel" if j == GC - 1 else None)
                m_sel[g] = m
                A, Bb, C = posA[:, 0:GC], posA[:, GC:2 * GC], posA[:, 2 * GC:3 * GC]
                m = do("vector", lambda e: e.tensor_copy(A, posf[:, r * GC:(r + 1) * GC]), m, inc="slot")
                do("vector", lambda e: e.tensor_single_scalar(Bb, A, 127, op=ALU.bitwise_and), m, inc="slot")
                m = do("vector", lambda e: e.tensor_single_scalar(C, A, 7, op=ALU.logical_shift_right), m, inc="slot")
                m_sl[g] = do("vector", lambda e: e.scalar_tensor_tensor(
                    posI[:, r * GC:(r + 1) * GC], Bb, float(ncol), C, ALU.mult, ALU.add), m,
                    *([m_scat[g - MR]] if g >= MR else []), inc="slot")

            def spread(g):
                m_oh[g] = do("vector", lambda e: e.tensor_scalar(OH[g % 2], offb[g % WR], iota_p[:, :], None, ALU.is_equal),
                             m_of[g], m_iotap, *([m_ohx[g - 2]] if g >= 2 else []), inc="spr")

            def expand_(g):
                r = g % MR
                ev = []
                for h in range(0, GC, 2):
                    i = take()
                    n = min(2, GC - h)
                    for j in range(n):
                        m = do("tensor", lambda e, i=i, j=j, h=h: e.matmul(
                            psum[i][0:PE_P, j * F:(j + 1) * F], OH[g % 2][:, (h + j) * PE_P:(h + j + 1) * PE_P], Win[g % WR],
                            start=True, stop=True), m_oh[g], m_w[g], *free[i], inc="exp" if j == n - 1 else None)
                    ev.append((i, h, n, m))
                m_ohx[g] = m
                M3 = msg[r].rearrange("p (j k) -> p j k", k=RW)
                for i, h, n, m in ev:
                    for j in range(n):
                        c = g * GC + h + j
                        m_e = do("scalar", lambda e, i=i, h=h, j=j, c=c: e.activation(
                            M3[:, h + j, 0:F], psum[i][0:PE_P, j * F:(j + 1) * F], ACT.Identity, scale=rec3[:, c, 2:3]),
                            m, mz, m_rec, *([m_scat[g - MR]] if g >= MR else []), inc="evc")
                    free[i] = [m_e]
                m_ev[g] = do("scalar", lambda e: e.activation(
                    M3[:, :, F:F + 3], rec3[:, g * GC:(g + 1) * GC, 0:3], ACT.Copy), m_rec, inc="evc")

            def send(g):
                r = g % MR
                for j in range(GC):
                    c = g * GC + j
                    row = msg[r][:, j * RW:(j + 1) * RW] if expand else rec[:, 4 * c:4 * c + 4]
                    m_scat[g] = do("gpsimd", lambda e, j=j, row=row: e.indirect_dma_start(
                        target, bass.IndirectOffsetOnAxis(ap=posI[:, r * GC + j:r * GC + j + 1], axis=0), row, None),
                        m_sl[g], *([m_filled] if g > g_fill else []), *([m_ev[g]] if expand else []), inc=f"scat{r}", by=16)

            if expand:
                turn[0], turn[1], turn[2] = 0, 3, 8
                load(0)
                load(1)
                spread(0)
            rank(0)
            rank(1)
            for g in range(NG):
                if g + 2 < NG:
                    rank(g + 2)
                slots(g)
                if expand:
                    if g + 1 < NG:
                        spread(g + 1)
                    expand_(g)
                    if g + 2 < NG:
                        load(g + 2)
                    if g % 3 == 0 and g // 3 < len(fills):
                        dma("sync", *fills[g // 3], m_zrow, inc="fillm")
                send(g)
            turn[0], turn[1], turn[2] = 0, 0, 8
            for k in range(3):
                free[k] = [m_sel[NG - 1]]
            return [m_scat[NG - 1 - k] for k in range(MR)] + [m_sel[NG - 1], m_sl[NG - 1]], m_rk[NG - 1]

        def transposes(src_cols, nblk, marks, name):
            ks = []
            for k in range(2):
                i = take()
                for j in range(nblk):
                    m = do("tensor", lambda e, i=i, j=j, k=k: e.transpose(
                        psum[i][:, j * R:(j + 1) * R], src_cols(j, k), ident[0:R, 0:R]), *marks, *free[i],
                        inc=name if j == nblk - 1 else None)
                ks.append((i, m))
            return ks

        def copy_out(eng, ks, dst, nblk, name, marks):
            for k, (i, m) in enumerate(ks):
                o = dst[:, k * 512:k * 512 + nblk * R]
                if eng == "scalar":
                    c = do(eng, lambda e, i=i, o=o: e.activation(o, psum[i][:, 0:nblk * R], ACT.Copy), m, *marks, inc=name)
                else:
                    c = do(eng, lambda e, i=i, o=o: e.tensor_copy(o, psum[i][:, 0:nblk * R]), m, *marks, inc=name)
                free[i] = [c]
            return c

        bst = small[:, 640:640 + 12 * len(SBS)].rearrange("p (m k) -> p m k", m=2)
        bn = small[:, 530:570]
        ns = len(SBS)

        def dense1_y(i, marks, aT, a_free, cp):
            b0, n = SBS[i]
            ks = transposes(lambda j, k: acc[0:R, (b0 + j) * F + k * P:(b0 + j) * F + (k + 1) * P], n, [*marks, m_ident], "d1_tr")
            mc = copy_out(cp, ks, aT[i % 2], n, "d1_cp", a_free.get(i - 2, []))
            for m_ in range(2):
                q = take()
                for k in range(2):
                    m = do("tensor", lambda e, q=q, m_=m_, k=k: e.matmul(
                        psum[q][:, 0:n * R], W1s[:, k, m_ * P:(m_ + 1) * P], aT[i % 2][:, k * 512:k * 512 + n * R],
                        start=k == 0, stop=k == 1), mc, m_W1, *free[q], inc="d1_mm" if k else None)
                a_free[i] = [m]
                yv = acc[:, b0 * F + m_ * n * R:b0 * F + (m_ + 1) * n * R]
                my = do("scalar", lambda e, q=q, yv=yv: e.activation(yv, psum[q][:, 0:n * R], ACT.Copy), m, inc="d1_y")
                free[q] = [my]
                my = do("vector", lambda e, m_=m_, yv=yv: e.bn_stats(bst[:, m_, 6 * i:6 * i + 6], yv), my, inc="d1_bs")
            return my

        def dense1_rest(m, aT, a_free):
            for m_ in range(2):
                m1 = do("vector", lambda e, m_=m_: e.bn_aggr(bn[:, 20 + 2 * m_:22 + 2 * m_], bst[:, m_, :]), m, inc="bn")
            mv = bn[:, 20:24].rearrange("p (m k) -> p m k", k=2)
            do("vector", lambda e: e.tensor_scalar(bn[:, 2:4], mv[:, :, 0], -1.0, None, ALU.mult), m1, inc="bn")
            m = do("vector", lambda e: e.tensor_scalar(bn[:, 6:8], mv[:, :, 1], EPS, None, ALU.add), inc="bn")
            m = do("scalar", lambda e: e.activation(bn[:, 8:10], bn[:, 6:8], ACT.Sqrt), m, inc="bn_rt")
            m = do("vector", lambda e: e.reciprocal(bn[:, 10:12], bn[:, 8:10]), m, inc="bn")
            m = do("vector", lambda e: e.tensor_tensor(bn[:, 12:14], bn[:, 10:12], gbT[:, 0:2], ALU.mult), m, m_gbT, inc="bn")
            m = do("vector", lambda e: e.tensor_tensor(bn[:, 14:16], bn[:, 12:14], bn[:, 2:4], ALU.mult), m, inc="bn")
            m_bn = do("vector", lambda e: e.tensor_tensor(bn[:, 16:18], bn[:, 14:16], gbT[:, 2:4], ALU.add), m, inc="bn")
            t_free = {}
            for i, (b0, n) in enumerate(SBS):
                for m_ in range(2):
                    yv = acc[:, b0 * F + m_ * n * R:b0 * F + (m_ + 1) * n * R]
                    mr = do("scalar", lambda e, m_=m_, yv=yv, i=i, n=n: e.activation(
                        aT[i % 2][:, m_ * 512:m_ * 512 + n * R], yv, ACT.Relu, bias=bn[:, 16 + m_:17 + m_], scale=bn[:, 12 + m_:13 + m_]),
                        m_bn, *a_free[ns - 1], *t_free.get(i - 2, []), inc="d1_h")
                for h in range(0, n, 2):
                    q = take()
                    for j in range(h, h + 2):
                        for m_ in range(2):
                            at = (j - h) * F + m_ * P
                            m = do("tensor", lambda e, q=q, at=at, i=i, m_=m_, j=j: e.transpose(
                                psum[q][0:R, at:at + P], aT[i % 2][:, m_ * 512 + j * R:m_ * 512 + (j + 1) * R], ident[:, :]),
                                mr, *free[q], inc="d1_bt" if (j > h and m_) else None)
                    t_free[i] = [m]
                    mh = do("vector", lambda e, q=q, b=b0 + h: e.tensor_copy(acc_b(b, 2), psum[q][0:R, :]), m, mr, inc="d1_hc")
                    free[q] = [mh]
                m_h2 = rows_("sync", h2[b0 * R:(b0 + n) * R, :].rearrange("(b p) f -> p b f", p=R),
                           acc_b(b0, n).rearrange("p (b f) -> p b f", f=F), mh, inc="st_h2")
            return m_h2, mh

        class Dense2:

            def __init__(self, cut, Z, tick=None, split=None):
                self.Z, self.split = Z, split
                if split:
                    self.wH, self.wL = ([split(f"w{j}{p}", 4096) for j in (1, 2)] for p in "HL")
                    self.tH, self.tL = ([split(f"t{j}{p}", 1024) for j in (1, 2)] for p in "HL")
                    self.hH, self.hL = ([split(f"h{j}{p}", 1024) for j in (1, 2)] for p in "HL")
                    self.hf = [cut(512) for _ in range(2)]
                    self.stage = cut(4096)
                    cut.at -= 4096
                    self.nh = 0
                else:
                    self.w = [cut(4096) for _ in range(2)]
                self.zT = cut(1024)
                self.xt = [cut(1024, R) for _ in range(2)]
                self.tt = cut(1024, R)
                self.tT = [cut(1024) for _ in range(2)]
                if not split:
                    self.hT = [cut(1024) for _ in range(2)]
                self.comb = [cut(32, R) for _ in range(2)]
                self.cT = cut(512, NEXP)
                self.rt = cut(256, R)
                self.fr, self.ready = {}, {}
                self.tick = tick or (lambda: None)

            def weights(self, *marks):
                for j, w in enumerate((w1, w2)):
                    v = w.rearrange("e (k p) f -> p e k f", p=P)
                    if not self.split:
                        self.m_ex = dma("sync", self.w[j].rearrange("p (e k f) -> p e k f", e=NEXP, k=2), v, *marks, inc="ld_ex")
                        continue
                    st = self.stage
                    m = dma("sync", st.rearrange("p (e k f) -> p e k f", e=NEXP, k=2), v, *marks, inc="ld_ex")
                    m = do("vector", lambda e, j=j: e.tensor_copy(self.wH[j][:, :], st), m, inc="wsp")
                    self.m_ex = do("vector", lambda e, j=j: e.tensor_tensor(
                        self.wL[j][:, :], st, self.wH[j][:, :].bitcast(F32), ALU.subtract), m, inc="wsp")
                    marks = [self.m_ex]

            def terms(self, j, i, ex):
                def w(t):
                    return t[:, ex * 512:(ex + 1) * 512].rearrange("p (k f) -> p k f", k=2)
                if not self.split:
                    return [(w(self.w[j]), self.tT[i % 2] if j == 0 else self.hT[ex % 2])]
                H, L = (self.tH[i % 2], self.tL[i % 2]) if j == 0 else (self.hH[ex % 2], self.hL[ex % 2])
                return [(w(self.wH[j]), H), (w(self.wL[j]), H), (w(self.wH[j]), L)]

            def first(self, i, m_agg, m_x0):
                fr, Zs, tick = self.fr, self.Z(i), self.tick
                b0, n = SBS[i]
                X, T, TT, C, zT, cT, rt = self.xt[i % 2], self.tt, self.tT[i % 2], self.comb[i % 2], self.zT, self.cT, self.rt
                mx = rows_("sync", X[:, 0:n * F].rearrange("p (b f) -> p b f", f=F),
                         x[b0 * R:(b0 + n) * R, :].rearrange("(b p) f -> p b f", p=R),
                         *m_x0, *fr.get(f"x{i % 2}", []), inc=f"ld_xt{i % 2}")
                ks = transposes(lambda j, k: Zs[:, j * F + k * P:j * F + (k + 1) * P], n, [*m_agg, m_ident], "d2_tr")
                m_tr = ks[-1][1]
                mc = copy_out("scalar", ks, zT, n, "d2_cp", [*m_x0, *fr.get("zT", [])])
                tick()
                yield
                for h in range(0, n, 2):
                    q = take()
                    for j in range(h, h + 2):
                        for k in range(2):
                            m = do("tensor", lambda e, q=q, j=j, h=h, k=k: e.matmul(
                                psum[q][0:R, (j - h) * F:(j - h + 1) * F], zT[:, k * 512 + j * R:k * 512 + (j + 1) * R], W2s[:, k, :],
                                start=k == 0, stop=k == 1), mc, m_W2, *free[q], inc="d2_z" if (j > h and k) else None)
                    fr["zT"] = [m]
                    mx1 = do("vector", lambda e, q=q, h=h: e.tensor_tensor(
                        X[:, h * F:(h + 2) * F], X[:, h * F:(h + 2) * F], psum[q][0:R, :], ALU.add), m, mx, inc="d2_x1")
                    free[q] = [mx1]
                    tick()
                yield
                v = small[0:R, 570:594]
                for j in range(n):
                    m = do("vector", lambda e, j=j: e.bn_stats(stats[:, 6 * j:6 * j + 6], X[:, j * F:(j + 1) * F]), mx1,
                           *fr.get("st", []), inc="d2_st")
                for j in range(n):
                    m1 = do("vector", lambda e, j=j: e.bn_aggr(v[:, 2 * j:2 * j + 2], stats[:, 6 * j:6 * j + 6]), m, *fr.get("v", []), inc="d2_st")
                fr["st"] = [m1]
                v3 = v[:, 0:8].rearrange("p (b k) -> p b k", k=2)
                m = do("vector", lambda e: e.tensor_scalar(v[:, 8:8 + n], v3[:, 0:n, 1], EPS, None, ALU.add), m1, inc="d2_st")
                m = do("scalar", lambda e: e.activation(v[:, 12:12 + n], v[:, 8:8 + n], ACT.Sqrt), m, inc="d2_sq")
                tick()
                m = do("vector", lambda e: e.reciprocal(v[:, 16:16 + n], v[:, 12:12 + n]), m, inc="d2_st")
                for j in range(n):
                    mt = do("vector", lambda e, j=j: e.tensor_scalar(
                        T[:, j * F:(j + 1) * F], X[:, j * F:(j + 1) * F], v[:, 2 * j:2 * j + 1], v[:, 16 + j:17 + j],
                        ALU.subtract, ALU.mult), m, *m_x0, *fr.get("T", []), inc="d2_t")
                fr["v"] = [mt]
                tick()
                mo = do("vector", lambda e: e.tensor_tensor(Zs[:, 0:n * F], X[:, 0:n * F], T[:, 0:n * F], ALU.add), mt, m_tr, inc="d2_o")
                fr[f"x{i % 2}"] = [mo]
                yield
                ks = transposes(lambda j, k: T[:, j * F + k * P:j * F + (k + 1) * P], n, [mt], "d2_tt")
                fr["T"] = [ks[-1][1], mo]
                mtT = copy_out("scalar", ks, TT, n, "d2_tc", [*m_x0, *fr.get(f"tT{i % 2}", [])])
                if self.split:
                    for k in range(2):
                        c_ = slice(k * 512, k * 512 + n * R)
                        mH = do("vector", lambda e, c_=c_: e.tensor_copy(self.tH[i % 2][:, c_], TT[:, c_]),
                                mtT, *fr.get(f"tT{i % 2}", []), inc="tsp")
                    for k in range(2):
                        c_ = slice(k * 512, k * 512 + n * R)
                        mtS = do("vector", lambda e, c_=c_: e.tensor_tensor(
                            self.tL[i % 2][:, c_], TT[:, c_], self.tH[i % 2][:, c_].bitcast(F32), ALU.subtract), mH, inc="tsp")
                tick()
                yield
                q = take()
                for j in range(n):
                    for k in range(2):
                        m = do("tensor", lambda e, q=q, j=j, k=k: e.matmul(
                            psum[q][0:R, j * 8:j * 8 + 8], TT[:, k * 512 + j * R:k * 512 + (j + 1) * R], rwT[:, k, :],
                            start=k == 0, stop=k == 1), mtT, m_rw, *free[q], inc="d2_lg" if (j == n - 1 and k) else None)
                L = psum[q][0:R, 0:8 * n].rearrange("p (b e) -> p b e", e=8)

                def r(at, w=1):
                    return rt[:, at:at + n * w] if w == 1 else rt[:, at:at + n * w].rearrange("p (b e) -> p b e", e=w)

                def wide(a):
                    return a.rearrange("p (b o) -> p b o", o=1).broadcast_to([R, n, 8])
                p8, m8 = r(8, 8), r(48, 8)
                ix, ixf = rt[:, 88:88 + 8 * n].bitcast(U32), r(128, 8)
                m = do("vector", lambda e: e.tensor_reduce(r(0), L, AX.X, ALU.max), m, *m_x0, *fr.get("rt", []), inc="rt")
                m = do("vector", lambda e: e.tensor_tensor(p8, L, wide(r(0)), ALU.subtract), m, inc="rt")
                free[q] = [m]
                m = do("scalar", lambda e: e.activation(p8, p8, ACT.Exp), m, inc="rt_e")
                tick()
                m = do("vector", lambda e: e.tensor_reduce(r(0), p8, AX.X, ALU.add), m, inc="rt")
                m = do("vector", lambda e: e.reciprocal(r(4), r(0)), m, inc="rt")
                m = do("vector", lambda e: e.tensor_tensor(p8, p8, wide(r(4)), ALU.mult), m, inc="rt")
                for j in range(n):
                    m1 = do("vector", lambda e, j=j: e.max(m8[:, j, :], p8[:, j, :]), m, inc="rt")
                for j in range(n):
                    m = do("vector", lambda e, j=j: e.max_index(ix[:, 8 * j:8 * j + 8], m8[:, j, :], p8[:, j, :]), m1, inc="rt")
                tick()
                do("vector", lambda e: e.tensor_copy(rt[:, 128:128 + 8 * n], ix), m, inc="rt")
                m = do("vector", lambda e: e.tensor_tensor(r(0), m8[:, :, 0], m8[:, :, 1], ALU.add), m, inc="rt")
                m = do("vector", lambda e: e.tensor_scalar(r(0), r(0), 1e-12, None, ALU.max), m, inc="rt")
                m = do("vector", lambda e: e.reciprocal(r(4), r(0)), m, inc="rt")
                m = do("vector", lambda e: e.tensor_tensor(m8, m8, wide(r(4)), ALU.mult), m, inc="rt")
                g0, g1 = r(168, 8), r(208, 8)
                for j in range(n):
                    do("vector", lambda e, j=j: e.tensor_scalar(g0[:, j, :], iota_f[0:R, 0:8], ixf[:, j, 0:1], m8[:, j, 0:1],
                                                                ALU.is_equal, ALU.mult), m, inc="rt")
                    m1 = do("vector", lambda e, j=j: e.tensor_scalar(g1[:, j, :], iota_f[0:R, 0:8], ixf[:, j, 1:2], m8[:, j, 1:2],
                                                                     ALU.is_equal, ALU.mult), inc="rt")
                mcb = do("vector", lambda e: e.tensor_tensor(C[:, 0:8 * n].rearrange("p (b e) -> p b e", e=8), g0, g1, ALU.add),
                         m1, *fr.get(f"c{i % 2}", []), inc="rt")
                fr["rt"] = [mcb]
                tick()
                yield
                q = take()
                for j in range(n):
                    m = do("tensor", lambda e, q=q, j=j: e.transpose(psum[q][0:8, j * R:(j + 1) * R], C[:, 8 * j:8 * j + 8], ident[0:R, 0:R]),
                           mcb, *free[q], inc="d2_ct" if j == n - 1 else None)
                m = do("scalar", lambda e, q=q: e.activation(cT[:, 0:n * R], psum[q][0:8, 0:n * R], ACT.Copy), m, *m_x0, *fr.get("cT", []), inc="d2_cc")
                free[q] = [m]
                yield
                for h in range(0, n, 2):
                    q = take()
                    for j in range(h, h + 2):
                        mb = do("tensor", lambda e, q=q, j=j, h=h: e.matmul(
                            psum[q][0:R, (j - h) * F:(j - h + 1) * F], cT[:, j * R:(j + 1) * R], b2s[:, :], start=True, stop=True),
                            m, m_b2, *free[q], inc="d2_b2" if j > h else None)
                    mo = do("vector", lambda e, q=q, h=h: e.tensor_tensor(Zs[:, h * F:(h + 2) * F], Zs[:, h * F:(h + 2) * F], psum[q][0:R, :], ALU.add),
                            mb, mo, inc="d2_o2")
                    free[q] = [mo]
                    tick()
                fr["cT"] = [mb]
                self.ready[i] = (mtS if self.split else mtT, mcb, mo)

            def experts(self, i, nxt):
                fr, Zs, tick = self.fr, self.Z(i), self.tick
                b0, n = SBS[i]
                mtT, mcb, mo0 = self.ready.pop(i)
                mo = [mo0]
                TT, C = self.tT[i % 2], self.comb[i % 2]
                up = {}

                def layer1(ex):
                    T_ = self.terms(0, i, ex)
                    for m_ in range(2):
                        q = take()
                        o = [(w, t, k) for w, t in T_ for k in range(2)]
                        for s_, (w, t, k) in enumerate(o):
                            m = do("tensor", lambda e, q=q, k=k, m_=m_, w=w, t=t, s_=s_: e.matmul(
                                psum[q][:, 0:n * R], w[:, k, m_ * P:(m_ + 1) * P], t[:, k * 512:k * 512 + n * R],
                                start=s_ == 0, stop=s_ == len(o) - 1), mtT, self.m_ex, *free[q], inc="l1" if s_ == len(o) - 1 else None)
                            if s_ % len(T_) == len(T_) - 1:
                                tick()
                        fr[f"tT{i % 2}"] = [m]
                        c_ = slice(m_ * 512, m_ * 512 + n * R)
                        old = fr.get(f"hT{ex % 2}", [])
                        if not self.split:
                            mg = do("scalar", lambda e, q=q, m_=m_, c_=c_: e.activation(
                                self.hT[ex % 2][:, c_], psum[q][:, 0:n * R], ACT.Gelu, bias=b1T[:, ex, m_:m_ + 1]),
                                m, m_b1, *old, inc="gelu")
                            free[q] = [mg]
                            continue
                        f = self.hf[self.nh % 2][:, 0:n * R]
                        H, L = self.hH[ex % 2][:, c_], self.hL[ex % 2][:, c_]
                        mg = do("scalar", lambda e, q=q, m_=m_, f=f: e.activation(
                            f, psum[q][:, 0:n * R], ACT.Gelu, bias=b1T[:, ex, m_:m_ + 1]),
                            m, m_b1, *fr.get(f"hf{self.nh % 2}", []), inc="gelu")
                        free[q] = [mg]
                        mg = do("scalar", lambda e, f=f, H=H: e.activation(H, f, ACT.Copy), mg, *old, inc="gelu")
                        mg = do("vector", lambda e, f=f, H=H, L=L: e.tensor_tensor(L, f, H.bitcast(F32), ALU.subtract),
                                mg, *old, inc="hsp")
                        fr[f"hf{self.nh % 2}"] = [mg]
                        self.nh += 1
                    up[ex] = mg

                def layer2(ex):
                    T_ = self.terms(1, i, ex)
                    new = None
                    for h in range(0, n, 2):
                        q = take()
                        for j in range(h, h + 2):
                            o = [(w, t, k) for w, t in T_ for k in range(2)]
                            for s_, (w, t, k) in enumerate(o):
                                m = do("tensor", lambda e, q=q, j=j, h=h, k=k, w=w, t=t, s_=s_: e.matmul(
                                    psum[q][0:R, (j - h) * F:(j - h + 1) * F], t[:, k * 512 + j * R:k * 512 + (j + 1) * R],
                                    w[:, k, :], start=s_ == 0, stop=s_ == len(o) - 1), up[ex], *free[q],
                                    inc="l2" if (j > h and s_ == len(o) - 1) else None)
                            tick()
                        fr[f"hT{ex % 2}"] = [m]
                        for j in range(h, h + 2):
                            a = Zs[:, j * F:(j + 1) * F]
                            new = do("vector", lambda e, q=q, j=j, h=h, a=a: e.scalar_tensor_tensor(
                                a, psum[q][0:R, (j - h) * F:(j - h + 1) * F], C[:, 8 * j + ex:8 * j + ex + 1], a,
                                ALU.mult, ALU.add), m, mo[0], mcb, inc="moe")
                        free[q] = [new]
                    mo[0] = new

                layer1(0)
                for ex in range(NEXP):
                    if ex + 1 < NEXP:
                        layer1(ex + 1)
                    next(nxt, None)
                    layer2(ex)
                for _ in nxt:
                    pass
                fr[f"c{i % 2}"] = [mo[0]]
                ms = rows_("sync", out[b0 * R:(b0 + n) * R, :].rearrange("(b p) f -> p b f", p=R),
                         Zs[:, 0:n * F].rearrange("p (b f) -> p b f", f=F), mo[0], inc=f"st_o{i % 4}")
                fr[f"Z{i % 4}"] = [ms]

            def stored(self):
                return [(f"st_o{k}", Q.count[f"st_o{k}"]) for k in range(4)]

        def general():
            for k in range(0, NCOL * 4, 1040):
                n = min(1040, NCOL * 4 - k)
                m_fill = dma("sync", tab_rows[:, k:k + n], zrow[:, 0:n], m_zrow, inc="fill")
            m = do("vector", lambda e: e.tensor_scalar(s_tot, cum[:, NG - 1:NG], 127.0, None, ALU.add), m_cum, inc="base")
            m = do("vector", lambda e: e.tensor_copy(s_nI, s_tot), m, inc="base")
            m = do("vector", lambda e: e.tensor_single_scalar(s_nI, s_nI, 7, op=ALU.logical_shift_right), m, inc="base")
            m = do("vector", lambda e: e.tensor_copy(s_n, s_nI), m, inc="base")
            m = do("tensor", lambda e: e.matmul(psum[0][0:NB, 0:1], lowT[0:NB, 0:NB], s_n, start=True, stop=True), m, *free[0], inc="scp")
            m = do("vector", lambda e: e.tensor_copy(s_sc, psum[0][0:NB, 0:1]), m, inc="base")
            free[0] = [m]
            m = do("vector", lambda e: e.tensor_scalar(s_sc128, s_sc, 128.0, None, ALU.mult), m, inc="base")
            m_gb = do("vector", lambda e: e.tensor_scalar(gb, gb, s_sc128, None, ALU.add), m, inc="base")
            scat, rk = scatter([m_gb], NCOL, tabd, m_fill, -1, False)
            half = NCOL // 2
            ci = bkf[0:NB, 0:half].bitcast(I32)
            ge = Bt[0][0:NB, 0:half]
            for k in range(2):
                mi = do("gpsimd", lambda e, k=k: e.iota(ci, pattern=[[1, half]], base=k * half, channel_multiplier=0),
                        *scat, *([("bmap", 1)] if k else []), inc="iotac")
                mm = do("vector", lambda e: e.tensor_scalar(ge, ci, s_sc, None, ALU.is_ge),
                        mi, rk, *([("bmap_p", 1)] if k else []), inc="bmap")
                for h in range(2):
                    pm = do("tensor", lambda e, h=h: e.matmul(psum[1 + h][0:1, 0:440], onesb[0:NB, 0:1], ge[:, h * 440:(h + 1) * 440],
                            start=True, stop=True), mm, *free[1 + h], *([("bmap", 2)] if k else []), inc="bmap_p" if h else None)
                for h in range(2):
                    at = k * half + h * 440
                    m_bk = do("vector", lambda e, h=h, at=at: e.tensor_scalar(
                        bkI[0:1, at:at + 440], psum[1 + h][0:1, 0:440], -1.0, float(F), ALU.add, ALU.mult), pm,
                        inc="bmap" if h else None)
            for k in range(8):
                free[k] = [*free[k], m_bk]

            cut = Cut(X0)
            tab = cut(NCOL * 4)
            tab3 = tab.rearrange("p (c k) -> p c k", k=4)
            GR, SR = 12, 6
            G = [cut(F) for i in range(GR)]
            S = [cut(R) for i in range(SR)]
            aT = [cut(1024) for i in range(2)]
            m = dma("sync", tab, tab_rows, *scat, m_bk, inc="ld_tab")
            m_tab = do("vector", lambda e: e.tensor_copy(tab3[:, :, 3].bitcast(I32), tab3[:, :, 0]), m, inc="tabi")

            def aggregate(t, hd, *ready):
                mg, ms, mm, ma, regs = {}, {}, {}, {}, {}
                wait("gpsimd", m_tab, *ready)
                wait("vector", m_tab, *ready)

                def load(c):
                    n = min(RL, CH - c)

                    def go(e):
                        _, v = nc.values_load_multi_w_load_instructions(
                            bkI[0:1, c:c + n], engines=[e.engine], min_val=0, max_val=(NB - 1) * F,
                            skip_runtime_bounds_check_because="a count of blocks, 1 to NB, less one, times F")
                        for k in range(n):
                            regs[c + k] = v[k]
                    Q.q["vector"].append(go)

                def add(c):
                    if c % RL == 0:
                        load(c)

                    def go(e):
                        a = acc[0:R, bass.ds(regs[c], F)]
                        return e.tensor_tensor(a, psum[c % PR][0:R, 0:F], a, ALU.add)
                    ma[c] = do("vector", go, mm[c], *([ma[c - 1]] if c else []), inc=f"{t}_add")

                LAG = 4
                for c in range(CH + LAG):
                    if c < CH:
                        prev = [mm[c - GR]] if c >= GR else []
                        mg[c] = do("gpsimd", lambda e, c=c: e.indirect_dma_start(
                            G[c % GR], None, hd, bass.IndirectOffsetOnAxis(ap=tab3[:, c, 3:4].bitcast(I32), axis=0)),
                            *prev, inc=f"gat{c % GR}", by=16)
                        prev = [mm[c - SR]] if c >= SR else []
                        ms[c] = do("vector", lambda e, c=c: e.tensor_scalar(
                            S[c % SR], iota_f[:, 0:R], tab3[:, c, 1:2], tab3[:, c, 2:3], ALU.is_equal, ALU.mult),
                            *prev, inc=f"{t}_sel")
                        prev = [ma[c - PR]] if c >= PR else free[c % PR]
                        mm[c] = do("tensor", lambda e, c=c: e.matmul(psum[c % PR][0:R, 0:F], S[c % SR], G[c % GR], start=True, stop=True),
                                   mg[c], ms[c], *prev, inc=f"{t}_mm")
                    if c >= LAG:
                        add(c - LAG)
                for k in range(8):
                    free[k] = [ma[CH - 1]]
                return mm[CH - 1], ma[CH - 1]

            pe1, agg1 = aggregate("a1", h1, m_h1, m_bk)
            a_free = {}
            for i in range(ns):
                my = dense1_y(i, [agg1], aT, a_free, "vector")
            m_h2, m_hc = dense1_rest(my, aT, a_free)
            pe2, agg2 = aggregate("a2", h2, m_h2, m_hc)
            D = Dense2(Cut(X0), lambda i: acc_b(*SBS[i]))
            D.weights(pe2, agg2)
            for _ in D.first(0, [agg2], [pe2, agg2]):
                pass
            for i in range(ns):
                D.experts(i, D.first(i + 1, [agg2], [agg2]) if i + 1 < ns else iter(()))
            wait("sync", *D.stored(), m_offd, m_W1)

        def ordered():
            m = do("vector", lambda e: e.tensor_scalar(s_sc128, iota_p[0:NB, :], float(KC * P), None, ALU.mult), m_cum, inc="base")
            m_gb = do("vector", lambda e: e.tensor_scalar(gb, gb, s_sc128, None, ALU.add), m, inc="base")
            scat, rk = scatter([m_gb], NCF, msgd, m_fillm, GF, True)
            tab3 = tabT[:, :].rearrange("p (c k) -> p c k", k=3)
            inner.close()
            stack = ExitStack()

            def st(name, n, dt=F32):
                return stack.enter_context(nc.sbuf_tensor(name, [P, n], dt))
            PC = 5
            pieces = [(b, k, n) for b in range(NB) for k, n in ((0, 5), (5, 4), (9, 5), (14, 4))]
            LR, HR = 6, 3
            L = [st(f"L{i}", PC * RW) for i in range(LR)]
            mH = [st(f"mH{i}", PC * F, FR) for i in range(HR)]
            mL = [st(f"mL{i}", PC * F, FR) for i in range(HR)]
            S = [st(f"S{i}", PC * R, FR) for i in range(HR)]
            aT = [st(f"aT{i}", 1024) for i in range(2)]
            for k in range(8):
                free[k] = [*free[k], rk]
            wait("scalar", *scat, rk)
            wait("vector", *scat, rk)
            wait("gpsimd", *scat, rk, m_fillm)
            wait("sync", *scat, rk)
            turn[0], turn[1], turn[2] = 0, 2, 8
            m_l, m_mm, m_cp, m_lo, a_free = {}, {}, {}, {}, {}

            def whole(u):
                return u % 3 == 1

            def load(u):
                b, k, n = pieces[u]
                m_l[u] = dma("sync", L[u % LR][:, 0:n * RW], msg3[:, b * KC + k:b * KC + k + n, :].rearrange("p k r -> p (k r)"),
                             *([m_cp[u - LR], *([m_mm[u - LR]] if whole(u - LR) else m_lo[u - LR])] if u >= LR else []), inc=f"ldm{u % LR}")

            def parts(u):
                b, k, n = pieces[u]
                L3 = L[u % LR].rearrange("p (k r) -> p k r", r=RW)[:, 0:n, :]
                H, Lo = (t[u % HR][:, 0:n * F].rearrange("p (k f) -> p k f", f=F) for t in (mH, mL))
                S3 = S[u % HR][:, 0:n * R].rearrange("p (k f) -> p k f", f=R)
                old = [m_mm[u - HR]] if u >= HR else []
                if not whole(u):
                    mh = do("scalar", lambda e: e.activation(H, L3[:, :, 0:F], ACT.Copy), m_l[u], *old, inc="r_hi")
                ms = do("vector", lambda e: e.tensor_tensor(
                    S3, iota_f[:, 0:R].rearrange("p (o f) -> p o f", o=1).broadcast_to([P, n, R]),
                    L3[:, :, F + 1:F + 2].broadcast_to([P, n, R]), ALU.is_equal), m_l[u], *old, inc="r_sel")
                if not whole(u):
                    m_lo[u] = [do(eng, lambda e, s_=s_: e.tensor_tensor(Lo[:, s_, :], L3[:, s_, 0:F], H[:, s_, :].bitcast(F32), ALU.subtract),
                                  mh, *old, inc=f"r_lo_{eng}") for eng, s_ in (("gpsimd", slice(0, 1)), ("vector", slice(1, n)))]
                m_cp[u] = do("gpsimd", lambda e: e.tensor_copy(tab3[:, b * KC + k:b * KC + k + n, :], L3[:, :, F:F + 3]),
                             m_l[u], ms, inc="r_tab")
                if whole(u):
                    return [(S3.bitcast(F32), L3[:, :, 0:F], [m_l[u]])], ms
                return [(S3, H, [mh]), (S3, Lo, m_lo[u])], ms

            for u in range(LR):
                load(u)
            nxt = parts(0)
            starts = {b: i for i, (b, n) in enumerate(SBS)}
            for u, (b, k0, n) in enumerate(pieces):
                terms, ms = nxt
                if u + 1 < len(pieces):
                    nxt = parts(u + 1)
                q = b % 2
                for h, (S3, part, mp) in enumerate(terms):
                    for k in range(n):
                        end = h == len(terms) - 1 and k == n - 1
                        m = do("tensor", lambda e, k=k, part=part, S3=S3, q=q, s0=k0 == 0 and k == 0 and h == 0, s1=end and k0 + n == KC: e.matmul(
                            psum[q][0:R, 0:F], S3[:, k, :], part[:, k, :], start=s0, stop=s1),
                            ms, *mp, *free[q], inc="r_mm" if end else None)
                m_mm[u] = m
                if u + LR < len(pieces):
                    load(u + LR)
                if k0 + n == KC:
                    m_ad = do("vector", lambda e, b=b, q=q: e.tensor_tensor(acc_b(b), acc_b(b), psum[q][0:R, 0:F], ALU.add), m, inc="r_add")
                    free[q] = [m_ad]
                    if b + 1 in starts:
                        pend = starts[b + 1] - 1, m_ad
                if k0 == PC and b and b in starts:
                    my = dense1_y(pend[0], [pend[1]], aT, a_free, "scalar")
            my = dense1_y(ns - 1, [m_ad], aT, a_free, "scalar")
            turn[0], turn[1], turn[2] = 0, 0, 8
            m_h2, m_hc = dense1_rest(my, aT, a_free)

            turn[0], turn[1], turn[2] = 0, 2, 8
            stack.close()
            phase.close()
            stack = ExitStack()

            def split(name, n):
                return stack.enter_context(nc.sbuf_tensor(name, [P, n], FR))
            cut = Cut(stack.enter_context(nc.sbuf_tensor("X1", [P, 15180], F32)))
            idx = tab3[:, :, 0].bitcast(I32)
            GR, SC, SR, HR = 12, 6, 3, 6
            LEAD = HR - 1
            G = [cut(F) for i in range(GR)]
            S2 = [split(f"s2{i}", SC * R) for i in range(SR)]
            gH = [split(f"gH{i}", F) for i in range(HR)]
            gL = [split(f"gL{i}", F) for i in range(HR)]
            Zb = [cut(1024, R) for i in range(4)]
            all_pe = ("d1_bt", Q.count["d1_bt"])
            m_idx = do("vector", lambda e: e.tensor_copy(idx, tab3[:, :, 0]), m_cp[len(pieces) - 1], m_h2, all_pe, inc="idx")
            wait("sync", m_h2, all_pe)
            wait("gpsimd", m_h2, all_pe, m_idx)
            wait("vector", m_h2, all_pe)
            wait("scalar", m_h2, all_pe, m_idx)
            mg, ms, mm, rel, mh, ml, m_z = {}, {}, {}, {}, {}, {}, {}

            def whole2(c):
                return c % 3 == 2

            def gather(c):
                if c >= GR:
                    wait("gpsimd", mm[c - GR] if whole2(c - GR) else ml[c - GR])
                mg[c] = do("gpsimd", lambda e: e.indirect_dma_start(
                    G[c % GR], None, h2, bass.IndirectOffsetOnAxis(ap=tab3[:, c, 0:1].bitcast(I32), axis=0)),
                    inc=f"gat{c % GR}", by=16)

            def prepare(c):
                s_ = c // SC
                if c % SC == 0:
                    ms[s_] = do("vector", lambda e: e.tensor_tensor(
                        S2[s_ % SR][:, :].rearrange("p (k f) -> p k f", f=R),
                        iota_f[:, 0:R].rearrange("p (o f) -> p o f", o=1).broadcast_to([P, SC, R]),
                        tab3[:, c:c + SC, 1:2].broadcast_to([P, SC, R]), ALU.is_equal),
                        *([mm[(s_ - SR) * SC + SC - 1]] if s_ >= SR else []), inc="g_sel")
                old = [mm[c - HR]] if c >= HR else []
                w_ = tab3[:, c, 2:3]
                if whole2(c):
                    mh[c] = do("scalar", lambda e: e.activation(G[c % GR], G[c % GR], ACT.Identity, scale=w_), mg[c], inc="g_hi")
                    return
                mh[c] = do("scalar", lambda e: e.activation(gH[c % HR][:, :], G[c % GR], ACT.Identity, scale=w_), mg[c], *old, inc="g_hi")
                ml[c] = do("vector", lambda e: e.scalar_tensor_tensor(
                    gL[c % HR][:, :], G[c % GR], w_, gH[c % HR][:, :].bitcast(F32), ALU.mult, ALU.subtract), mh[c], *old, inc="g_lo")

            for c in range(GR):
                gather(c)
            for c in range(LEAD):
                prepare(c)

            def chunks(i):
                b0, n = SBS[i]
                Zs = Zb[i % 4]
                old = D.fr.get(f"Z{i % 4}", [])
                m_s = rows_("sync", Zs[:, 0:n * F].rearrange("p (b f) -> p b f", f=F),
                          h2[b0 * R:(b0 + n) * R, :].rearrange("(b p) f -> p b f", p=R), *old, inc=f"ld_z{i % 4}")
                for b in range(b0, b0 + n):
                    q = b % 2
                    for k in range(KC):
                        c = b * KC + k
                        if c + LEAD < NCF:
                            prepare(c + LEAD)
                        Sc = S2[c // SC % SR][:, c % SC * R:(c % SC + 1) * R]
                        if whole2(c):
                            terms = [(Sc.bitcast(F32), G[c % GR], mh[c])]
                        else:
                            terms = [(Sc, gH[c % HR][:, :], mh[c]), (Sc, gL[c % HR][:, :], ml[c])]
                        for h, (sel_, row, mr) in enumerate(terms):
                            end = h == len(terms) - 1
                            mm[c] = do("tensor", lambda e, sel_=sel_, row=row, q=q, s0=k == 0 and h == 0, s1=end and k == KC - 1: e.matmul(
                                psum[q][0:R, 0:F], sel_, row, start=s0, stop=s1),
                                mr, ms[c // SC], *free[q], inc="g_mm" if end else None)
                        if c + GR < NCF:
                            gather(c + GR)
                        if k < KC - 1:
                            yield
                    j = b - b0
                    m_z[i] = do("vector", lambda e, j=j, q=q: e.tensor_tensor(
                        Zs[:, j * F:(j + 1) * F], Zs[:, j * F:(j + 1) * F], psum[q][0:R, 0:F], ALU.add), mm[c], m_s, inc="g_add")
                    free[q] = [m_z[i]]
                    yield

            flow = [iter(())]
            D = Dense2(cut, lambda i: Zb[i % 4][:, 0:SBS[i][1] * F], lambda: next(flow[0], None), split)
            D.weights()
            for t in range(ns + 2):
                flow[0] = chunks(t) if t < ns else iter(())
                nxt = D.first(t - 1, [m_z[t - 1]], [D.m_ex]) if 1 <= t <= ns else iter(())
                if t >= 2:
                    D.experts(t - 2, nxt)
                for _ in nxt:
                    pass
                for _ in flow[0]:
                    pass
            wait("sync", *D.stored(), m_fillm, m_offd)
            stack.close()

        fast = Q.path(ordered)
        for k in range(8):
            free[k] = [m_cum, m_pre, m_flag]
        turn[0], turn[1], turn[2] = 0, 0, 8
        slow = Q.path(general)
        Q.run(ctx.enter_context(nc.Block()), nc, flagI, m_flag, fast, slow)


_INS = ["x", "src", "dst", "edge_weight", "L0_gnn_W1", "L0_gnn_W2", "L0_gnn_gamma", "L0_gnn_beta",
        "L0_ffn_router_w", "L0_ffn_w1", "L0_ffn_b1", "L0_ffn_w2", "L0_ffn_b2"]


def kernel(**inputs):
    import numpy as np
    import concourse.bacc as bacc
    from concourse.bass_utils import run_bass_kernel_spmd

    nc = bacc.Bacc("TRN2", target_bir_lowering=False, num_devices=1)
    arrays, args = {}, []
    for name in _INS:
        a = np.ascontiguousarray(inputs[name])
        arrays[f"in_{name}"] = a
        args.append(nc.dram_tensor(f"in_{name}", a.shape, mybir.dt.from_np(a.dtype), kind="ExternalInput").ap())
    out = nc.dram_tensor("out_0", (N, F), F32, kind="ExternalOutput").ap()
    build(nc, *args, out)
    r = run_bass_kernel_spmd(nc, [arrays], core_ids=[0])
    return r.results[0]["out_0"]
```
